# Optimizing a Trainium2 kernel written in Bass

```python
import numpy as np
import jax
import jax.numpy as jnp

def _softmax(x, axis=-1):
    return jax.nn.softmax(x, axis=axis)
def _gelu(x):
    return jax.nn.gelu(x, approximate=True)
def _silu(x):
    return jax.nn.silu(x)
def _sigmoid(x):
    return jax.nn.sigmoid(x)
def _layernorm(x, axis=-1, eps=1e-5):
    m = jnp.mean(x, axis=axis, keepdims=True)
    v = jnp.var(x, axis=axis, keepdims=True)
    return (x - m) / jnp.sqrt(v + eps)
def _scatter_add(tgt, idx, src, axis=0):
    return tgt.at[idx].add(src)
def _segment_sum(src, seg, n):
    return jax.ops.segment_sum(src, seg, n)

kernel_name = 'mk_conv_preact_d2_conv_nhwc96_4be4b3'

def setup_inputs(seed: int = 0):
    np.random.seed(seed)
    _w = jnp.asarray
    def _rec_inputs():
        import jax
        import jax.numpy as jnp
        _gk = jax.random.key(seed)
        x = -0.000357 + 1 * jax.random.normal(jax.random.fold_in(_gk, 1), (64, 56, 56, 96), jnp.float32)
        return x
    x = _rec_inputs()
    def _L0_conv_setup():
        import jax, jax.numpy as jnp
        import numpy as np
        WS = 7
        HEADS = 3
        DIM = 96
        HEAD_DIM = DIM // HEADS
        SCALE = HEAD_DIM ** (-0.5)

        def _rel_pos_index(ws: int) -> np.ndarray:
            coords = np.stack(np.meshgrid(np.arange(ws), np.arange(ws), indexing='ij'))
            cf = coords.reshape(2, -1)
            rel = cf[:, :, None] - cf[:, None, :]
            rel = rel.transpose(1, 2, 0).astype(np.int64)
            rel[:, :, 0] += ws - 1
            rel[:, :, 1] += ws - 1
            rel[:, :, 0] *= 2 * ws - 1
            return rel.sum(-1).reshape(-1)
        _REL_IDX = _rel_pos_index(WS)
        key = jax.random.key(seed)
        ks = jax.random.split(key, 6)
        return {'x': jax.random.normal(ks[0], (64, 56, 56, DIM), jnp.float32), 'w_qkv': jax.random.normal(ks[1], (DIM, 3 * DIM), jnp.float32) * 0.02, 'b_qkv': jax.random.normal(ks[2], (3 * DIM,), jnp.float32) * 0.02, 'rel_pos': jax.random.normal(ks[3], (HEADS, (2 * WS - 1) ** 2), jnp.float32) * 0.02, 'w_out': jax.random.normal(ks[4], (DIM, DIM), jnp.float32) * 0.02, 'b_out': jax.random.normal(ks[5], (DIM,), jnp.float32) * 0.02}
    _L0_conv_all = _L0_conv_setup()
    _L0_conv_in = {k: v for k, v in _L0_conv_all.items() if k in ('w_qkv', 'b_qkv', 'rel_pos', 'w_out', 'b_out', )}
    del _L0_conv_all

    def _L1_conv_setup():
        import jax, jax.numpy as jnp
        import numpy as np
        D_MODEL, D_STATE, D_CONV = (96, 16, 3)
        D_INNER = int(2.0 * D_MODEL)
        DT_RANK = -(-D_MODEL // 16)
        K = 4

        def _ss2d(x, in_proj_w, conv_w, conv_b, x_proj_weight, dt_projs_weight, dt_projs_bias, A_logs, Ds, ln_w, ln_b, out_proj_w):
            B, H, W, _ = x.shape
            L = H * W
            xz = x @ in_proj_w.T
            xx, z = jnp.split(xz, 2, axis=-1)
            xc = xx.transpose(0, 3, 1, 2)
            xc = jax.lax.conv_general_dilated(xc, conv_w, (1, 1), 'SAME', dimension_numbers=('NCHW', 'OIHW', 'NCHW'), feature_group_count=D_INNER) + conv_b[None, :, None, None]
            xc = jax.nn.silu(xc)
            x_hw = xc.reshape(B, D_INNER, L)
            x_wh = xc.transpose(0, 1, 3, 2).reshape(B, D_INNER, L)
            x_hwwh = jnp.stack([x_hw, x_wh], axis=1)
            xs = jnp.concatenate([x_hwwh, jnp.flip(x_hwwh, -1)], axis=1)
            x_dbl = jnp.einsum('bkdl,kcd->bkcl', xs, x_proj_weight)
            dts = x_dbl[:, :, :DT_RANK]
            Bs = x_dbl[:, :, DT_RANK:DT_RANK + D_STATE]
            Cs = x_dbl[:, :, DT_RANK + D_STATE:]
            dts = jnp.einsum('bkrl,kdr->bkdl', dts, dt_projs_weight)
            delta = jax.nn.softplus(dts + dt_projs_bias[None, :, :, None])
            As = -jnp.exp(A_logs).reshape(K, D_INNER, D_STATE)

            def step(h, inp):
                u_t, d_t, B_t, C_t = inp
                dA = jnp.exp(d_t[..., None] * As)
                h = dA * h + d_t[..., None] * B_t[:, :, None, :] * u_t[..., None]
                y = jnp.einsum('bkdn,bkn->bkd', h, C_t)
                return (h, y)
            h0 = jnp.zeros((B, K, D_INNER, D_STATE), xs.dtype)
            inputs = (xs.transpose(3, 0, 1, 2), delta.transpose(3, 0, 1, 2), Bs.transpose(3, 0, 1, 2), Cs.transpose(3, 0, 1, 2))
            _, ys = jax.lax.scan(step, h0, inputs)
            out_y = ys.transpose(1, 2, 3, 0) + Ds.reshape(K, D_INNER)[None, :, :, None] * xs
            inv_y = jnp.flip(out_y[:, 2:4], -1)
            wh_y = out_y[:, 1].reshape(B, D_INNER, W, H).transpose(0, 1, 3, 2).reshape(B, D_INNER, L)
            invwh_y = inv_y[:, 1].reshape(B, D_INNER, W, H).transpose(0, 1, 3, 2).reshape(B, D_INNER, L)
            y = out_y[:, 0] + inv_y[:, 0] + wh_y + invwh_y
            y = y.transpose(0, 2, 1).reshape(B, H, W, D_INNER)
            mu = y.mean(-1, keepdims=True)
            var = ((y - mu) ** 2).mean(-1, keepdims=True)
            y = (y - mu) * jax.lax.rsqrt(var + 1e-05) * ln_w + ln_b
            y = y * jax.nn.silu(z)
            return y @ out_proj_w.T
        key = jax.random.key(seed)
        ks = jax.random.split(key, 8)
        B, H, W = (8, 64, 64)
        x = jax.random.normal(ks[0], (B, H, W, D_MODEL), jnp.float32)
        in_proj_w = jax.random.normal(ks[1], (2 * D_INNER, D_MODEL), jnp.float32) * 0.05
        conv_w = jax.random.normal(ks[2], (D_INNER, 1, D_CONV, D_CONV), jnp.float32) * 0.1
        conv_b = jnp.zeros((D_INNER,), jnp.float32)
        x_proj_weight = jax.random.normal(ks[3], (K, DT_RANK + 2 * D_STATE, D_INNER), jnp.float32) * 0.05
        dt_projs_weight = jax.random.normal(ks[4], (K, D_INNER, DT_RANK), jnp.float32) * DT_RANK ** (-0.5)
        dt0 = 0.01
        dt_projs_bias = jnp.full((K, D_INNER), float(np.log(np.expm1(dt0))), jnp.float32)
        A_logs = jnp.log(jnp.tile(jnp.arange(1, D_STATE + 1, dtype=jnp.float32), (K * D_INNER, 1)))
        Ds = jnp.ones((K * D_INNER,), jnp.float32)
        ln_w = jnp.ones((D_INNER,), jnp.float32)
        ln_b = jnp.zeros((D_INNER,), jnp.float32)
        out_proj_w = jax.random.normal(ks[5], (D_MODEL, D_INNER), jnp.float32) * 0.05
        return dict(x=x, in_proj_w=in_proj_w, conv_w=conv_w, conv_b=conv_b, x_proj_weight=x_proj_weight, dt_projs_weight=dt_projs_weight, dt_projs_bias=dt_projs_bias, A_logs=A_logs, Ds=Ds, ln_w=ln_w, ln_b=ln_b, out_proj_w=out_proj_w)
    _L1_conv_all = _L1_conv_setup()
    _L1_conv_in = {k: v for k, v in _L1_conv_all.items() if k in ('in_proj_w', 'conv_w', 'conv_b', 'x_proj_weight', 'dt_projs_weight', 'dt_projs_bias', 'A_logs', 'Ds', 'ln_w', 'ln_b', 'out_proj_w', )}
    del _L1_conv_all

    return {
        "x": x,
        "L0_conv_w_qkv": _L0_conv_in["w_qkv"],
        "L0_conv_b_qkv": _L0_conv_in["b_qkv"],
        "L0_conv_rel_pos": _L0_conv_in["rel_pos"],
        "L0_conv_w_out": _L0_conv_in["w_out"],
        "L0_conv_b_out": _L0_conv_in["b_out"],
        "L1_conv_in_proj_w": _L1_conv_in["in_proj_w"],
        "L1_conv_conv_w": _L1_conv_in["conv_w"],
        "L1_conv_conv_b": _L1_conv_in["conv_b"],
        "L1_conv_x_proj_weight": _L1_conv_in["x_proj_weight"],
        "L1_conv_dt_projs_weight": _L1_conv_in["dt_projs_weight"],
        "L1_conv_dt_projs_bias": _L1_conv_in["dt_projs_bias"],
        "L1_conv_A_logs": _L1_conv_in["A_logs"],
        "L1_conv_Ds": _L1_conv_in["Ds"],
        "L1_conv_ln_w": _L1_conv_in["ln_w"],
        "L1_conv_ln_b": _L1_conv_in["ln_b"],
        "L1_conv_out_proj_w": _L1_conv_in["out_proj_w"],
    }

def reference(x, L0_conv_w_qkv, L0_conv_b_qkv, L0_conv_rel_pos, L0_conv_w_out, L0_conv_b_out, L1_conv_in_proj_w, L1_conv_conv_w, L1_conv_conv_b, L1_conv_x_proj_weight, L1_conv_dt_projs_weight, L1_conv_dt_projs_bias, L1_conv_A_logs, L1_conv_Ds, L1_conv_ln_w, L1_conv_ln_b, L1_conv_out_proj_w):
    import jax
    import jax.numpy as jnp
    def _L0_conv_ref(x, w_qkv, b_qkv, rel_pos, w_out, b_out):
        import jax, jax.numpy as jnp
        import numpy as np
        WS = 7
        HEADS = 3
        DIM = 96
        HEAD_DIM = DIM // HEADS
        SCALE = HEAD_DIM ** (-0.5)

        def _rel_pos_index(ws: int) -> np.ndarray:
            coords = np.stack(np.meshgrid(np.arange(ws), np.arange(ws), indexing='ij'))
            cf = coords.reshape(2, -1)
            rel = cf[:, :, None] - cf[:, None, :]
            rel = rel.transpose(1, 2, 0).astype(np.int64)
            rel[:, :, 0] += ws - 1
            rel[:, :, 1] += ws - 1
            rel[:, :, 0] *= 2 * ws - 1
            return rel.sum(-1).reshape(-1)
        _REL_IDX = _rel_pos_index(WS)
        b, H, W, c = x.shape
        h, w = (H // WS, W // WS)
        n = WS * WS
        xw = x.reshape(b, WS, h, WS, w, c).transpose(0, 2, 4, 1, 3, 5).reshape(b, h, w, n, c)
        qkv = xw @ w_qkv + b_qkv
        q, k, v = jnp.split(qkv, 3, axis=-1)

        def to_heads(t):
            return t.reshape(b, h, w, n, HEADS, HEAD_DIM).transpose(0, 4, 1, 2, 3, 5)
        q, k, v = (to_heads(q) * SCALE, to_heads(k), to_heads(v))
        sim = jnp.einsum('bghwnd,bghwmd->bghwnm', q, k)
        bias = rel_pos[:, _REL_IDX].reshape(HEADS, n, n)
        sim = sim + bias[None, :, None, None]
        att = jax.nn.softmax(sim, axis=-1)
        out = jnp.einsum('bghwnm,bghwmd->bghwnd', att, v)
        out = out.transpose(0, 2, 3, 4, 1, 5).reshape(b, h, w, n, c)
        out = out.reshape(b, h, w, WS, WS, c).transpose(0, 3, 1, 4, 2, 5).reshape(b, H, W, c)
        return out @ w_out + b_out

    def _L1_conv_ref(x, in_proj_w, conv_w, conv_b, x_proj_weight, dt_projs_weight, dt_projs_bias, A_logs, Ds, ln_w, ln_b, out_proj_w):
        import jax, jax.numpy as jnp
        import numpy as np
        D_MODEL, D_STATE, D_CONV = (96, 16, 3)
        D_INNER = int(2.0 * D_MODEL)
        DT_RANK = -(-D_MODEL // 16)
        K = 4

        def _ss2d(x, in_proj_w, conv_w, conv_b, x_proj_weight, dt_projs_weight, dt_projs_bias, A_logs, Ds, ln_w, ln_b, out_proj_w):
            B, H, W, _ = x.shape
            L = H * W
            xz = x @ in_proj_w.T
            xx, z = jnp.split(xz, 2, axis=-1)
            xc = xx.transpose(0, 3, 1, 2)
            xc = jax.lax.conv_general_dilated(xc, conv_w, (1, 1), 'SAME', dimension_numbers=('NCHW', 'OIHW', 'NCHW'), feature_group_count=D_INNER) + conv_b[None, :, None, None]
            xc = jax.nn.silu(xc)
            x_hw = xc.reshape(B, D_INNER, L)
            x_wh = xc.transpose(0, 1, 3, 2).reshape(B, D_INNER, L)
            x_hwwh = jnp.stack([x_hw, x_wh], axis=1)
            xs = jnp.concatenate([x_hwwh, jnp.flip(x_hwwh, -1)], axis=1)
            x_dbl = jnp.einsum('bkdl,kcd->bkcl', xs, x_proj_weight)
            dts = x_dbl[:, :, :DT_RANK]
            Bs = x_dbl[:, :, DT_RANK:DT_RANK + D_STATE]
            Cs = x_dbl[:, :, DT_RANK + D_STATE:]
            dts = jnp.einsum('bkrl,kdr->bkdl', dts, dt_projs_weight)
            delta = jax.nn.softplus(dts + dt_projs_bias[None, :, :, None])
            As = -jnp.exp(A_logs).reshape(K, D_INNER, D_STATE)

            def step(h, inp):
                u_t, d_t, B_t, C_t = inp
                dA = jnp.exp(d_t[..., None] * As)
                h = dA * h + d_t[..., None] * B_t[:, :, None, :] * u_t[..., None]
                y = jnp.einsum('bkdn,bkn->bkd', h, C_t)
                return (h, y)
            h0 = jnp.zeros((B, K, D_INNER, D_STATE), xs.dtype)
            inputs = (xs.transpose(3, 0, 1, 2), delta.transpose(3, 0, 1, 2), Bs.transpose(3, 0, 1, 2), Cs.transpose(3, 0, 1, 2))
            _, ys = jax.lax.scan(step, h0, inputs)
            out_y = ys.transpose(1, 2, 3, 0) + Ds.reshape(K, D_INNER)[None, :, :, None] * xs
            inv_y = jnp.flip(out_y[:, 2:4], -1)
            wh_y = out_y[:, 1].reshape(B, D_INNER, W, H).transpose(0, 1, 3, 2).reshape(B, D_INNER, L)
            invwh_y = inv_y[:, 1].reshape(B, D_INNER, W, H).transpose(0, 1, 3, 2).reshape(B, D_INNER, L)
            y = out_y[:, 0] + inv_y[:, 0] + wh_y + invwh_y
            y = y.transpose(0, 2, 1).reshape(B, H, W, D_INNER)
            mu = y.mean(-1, keepdims=True)
            var = ((y - mu) ** 2).mean(-1, keepdims=True)
            y = (y - mu) * jax.lax.rsqrt(var + 1e-05) * ln_w + ln_b
            y = y * jax.nn.silu(z)
            return y @ out_proj_w.T
        return _ss2d(x, in_proj_w, conv_w, conv_b, x_proj_weight, dt_projs_weight, dt_projs_bias, A_logs, Ds, ln_w, ln_b, out_proj_w)

    def _gn(v, G=32, eps=1e-5):
        B_, H_, W_, C_ = v.shape
        g = v.reshape(B_, H_, W_, G, C_ // G)
        m = jnp.mean(g, axis=(1, 2, 4), keepdims=True)
        s = jnp.var(g, axis=(1, 2, 4), keepdims=True)
        return ((g - m) / jnp.sqrt(s + eps)).reshape(v.shape)

    def _ln_c(v, eps=1e-6):
        m = jnp.mean(v, axis=-1, keepdims=True)
        s = jnp.var(v, axis=-1, keepdims=True)
        return (v - m) / jnp.sqrt(s + eps)

    def _ln_t(v, eps=1e-5):
        m = jnp.mean(v, axis=-1, keepdims=True)
        s = jnp.var(v, axis=-1, keepdims=True)
        return (v - m) / jnp.sqrt(s + eps)

    def _to_tokens(v):
        B_, H_, W_, C_ = v.shape
        return v.reshape(B_, H_ * W_, C_)
    def _from_tokens(t, like):
        return t.reshape(like.shape)

    x = x + _L0_conv_ref(_gn(x), L0_conv_w_qkv, L0_conv_b_qkv, L0_conv_rel_pos, L0_conv_w_out, L0_conv_b_out)
    x = x + _L1_conv_ref(_gn(x), L1_conv_in_proj_w, L1_conv_conv_w, L1_conv_conv_b, L1_conv_x_proj_weight, L1_conv_dt_projs_weight, L1_conv_dt_projs_bias, L1_conv_A_logs, L1_conv_Ds, L1_conv_ln_w, L1_conv_ln_b, L1_conv_out_proj_w)
    return x


_drawn_inputs = setup_inputs


def setup_inputs(seed=0):
    import zlib

    import numpy as np

    out = dict(_drawn_inputs(seed))
    spreads = {'L1_conv_conv_b': (0.0, 0.1),
     'L1_conv_dt_projs_bias': (-4.600165843963623, 0.6),
     'L1_conv_Ds': (1.0, 0.6),
     'L1_conv_ln_w': (1.0, 0.6),
     'L1_conv_ln_b': (0.0, 0.425)}
    factors = {'L0_conv_w_qkv': 8.0,
     'L0_conv_b_qkv': 8.0,
     'L0_conv_rel_pos': 8.0,
     'L0_conv_w_out': 7.988,
     'L0_conv_b_out': 2.733,
     'L1_conv_x_proj_weight': 8.0,
     'L1_conv_dt_projs_weight': 8.0,
     'L1_conv_A_logs': 28.161}
    for name, (base, spread) in spreads.items():
        noise = np.random.default_rng([zlib.crc32(name.encode()), seed]).standard_normal(out[name].shape)
        drawn = base * np.exp(spread * noise) if base else spread * noise
        out[name] = jnp.asarray(drawn.astype(out[name].dtype))
    for name, factor in factors.items():
        out[name] = (out[name] * factor).astype(out[name].dtype)
    return out
```

```python
from contextlib import ExitStack

import numpy as np
import concourse.bass as bass
from concourse import mybir

F32 = mybir.dt.float32
F32R = mybir.dt.float32r
ALU = mybir.AluOpType
ACT = mybir.ActivationFunctionType
AX = mybir.AxisListType

IMAGES, SIDE, DIM = 64, 56, 96
PIX = SIDE * SIDE
GROUP = 3
WS, HEADS = 7, 3
HEAD_DIM = DIM // HEADS
WIN = SIDE // WS
TOK = WS * WS
ROWPIX = WIN * TOK
PAIRS = WIN // 2
SCALE = HEAD_DIM ** (-0.5)
INNER, STATE, RANK, DIRS = 192, 16, 6, 4
HALVES = INNER // DIM
CH = 448
CHUNKS = PIX // CH
LINES = CH // SIDE
DGROUPS = INNER // 32
QUADS = STATE // 4
TILES = DGROUPS * QUADS
GN_EPS = LN_EPS = 1e-5
PADDED = SIDE + 2
B_ROW, C_ROW, XD_ROWS = 32, 64, 80
SOFTPLUS_TOP = 40.0

ITEMS = [("proj", 0, 0), ("dt", 0, 3), ("rep", 0, 7), ("rep", 4, 8), ("rep", 1, 9), ("rep", 5, 10),
         ("dt", 1, 12), ("rep", 2, 16), ("rep", 6, 17), ("rep", 3, 18), ("rep", 7, 19)]
PREPS = len(ITEMS)
DT_ITEM = [ITEMS.index(i) for i in ITEMS if i[0] == "dt"]
DT_SLOT = [ITEMS[n][2] for n in DT_ITEM]
HIGH_SLOT = [DT_SLOT[0] + 4, 19]


def build(nc, a, images):
    with ExitStack() as ctx:
        def sb(name, shape, dtype=F32):
            return ctx.enter_context(nc.sbuf_tensor(name, shape, dtype))

        def sem(name):
            return ctx.enter_context(nc.semaphore(name))

        rep_sel = sb("rep_sel", [DIM, 3, 128], F32R)
        bc_sel = sb("bc_sel", [XD_ROWS, 8, 128], F32R)
        sum_sel = sb("sum_sel", [128, 3, DIM])
        ident = sb("ident", [128, 128])
        group_avg = sb("group_avg", [DIM, DIM])
        inner_avg = sb("inner_avg", [DIM, DIM])
        w_in = sb("w_in", [DIM, 2 * INNER])
        conv_w = sb("conv_w", [DIM, HALVES, 9])
        conv_b = sb("conv_b", [DIM, HALVES])
        xproj = sb("xproj", [DIM, DIRS, HALVES, XD_ROWS])
        dt_w = sb("dt_w", [XD_ROWS, DIRS, INNER])
        dt_b = sb("dt_b", [DIM, DIRS, HALVES])
        a_neg = sb("a_neg", [128, DIRS, TILES])
        d_skip = sb("d_skip", [DIM, HALVES, DIRS])
        d_sum = sb("d_sum", [DIM, HALVES])
        ln_w = sb("ln_w", [DIM, HALVES])
        ln_b = sb("ln_b", [DIM, HALVES])
        w_out2 = sb("w_out2", [DIM, HALVES, DIM])
        eps = sb("eps", [128, 1])
        stats = sb("stats", [DIM, CHUNKS, 6])
        mv = sb("mv", [DIM, 2])
        gm = sb("gm", [DIM, 4])
        image = sb("image", [DIM, 2 * PIX])
        psum = ctx.enter_context(nc.psum_tensor("psum", [128, 8, 512], F32))

        s_w = sem("s_w")
        s_const = sem("s_const")
        s_load = [sem("s_load0"), sem("s_load1")]
        s_stored = [sem("s_stored0"), sem("s_stored1")]
        s_gate = sem("s_gate")

        loads = [(sum_sel, "sum_sel"), (ident, "ident"),
                 (group_avg, "group_avg"), (inner_avg, "inner_avg"), (w_in, "w_in"), (conv_w, "conv_w"),
                 (conv_b, "conv_b"), (xproj, "xproj"), (dt_w, "dt_w"), (dt_b, "dt_b"), (a_neg, "a_log"),
                 (d_skip, "d_skip"), (ln_w, "ln_w"), (ln_b, "ln_b"), (w_out2, "w_out2")]

        def img(par):
            return image[:, bass.ds(par * PIX, PIX)]

        def image_loop(eng, body):
            with eng.Fori(0, images // 2) as i:
                for par in range(2):
                    body(i, i * 2 + par, par)

        s_chan = sem("s_chan")
        s_grp = sem("s_grp")
        s_gvar = sem("s_gvar")
        s_rstd = sem("s_rstd")
        s_norm = sem("s_norm")
        s_dv = sem("s_dv")
        s_lg = sem("s_lg")

        def gn_vector(v, b, par, ready):
            ready()
            for c in range(CHUNKS):
                ins = nc.vector.bn_stats(stats[:, c, :], img(par)[:, c * CH:(c + 1) * CH])
            ins.then_inc(s_dv, 1)
            v.wait_ge(s_dv, b * 6 + 1)
            v.sem_inc(s_gate, 1)
            nc.vector.bn_aggr(mv[:, :], stats[:, :, :].rearrange("p c s -> p (c s)")).then_inc(s_dv, 1)
            v.wait_ge(s_dv, b * 6 + 2)
            nc.vector.tensor_tensor(gm[:, 0:1], mv[:, 0:1], mv[:, 0:1], ALU.mult).then_inc(s_dv, 1)
            v.wait_ge(s_dv, b * 6 + 3)
            nc.vector.tensor_tensor(mv[:, 1:2], mv[:, 1:2], gm[:, 0:1], ALU.add).then_inc(s_chan, 1)
            v.wait_ge(s_grp, b + 1)
            nc.vector.tensor_copy(gm[:, 0:2], psum[0:DIM, 7, 448:450]).then_inc(s_dv, 1)
            v.wait_ge(s_dv, b * 6 + 4)
            nc.vector.tensor_tensor(gm[:, 2:3], gm[:, 0:1], gm[:, 0:1], ALU.mult).then_inc(s_dv, 1)
            v.wait_ge(s_dv, b * 6 + 5)
            nc.vector.tensor_tensor(gm[:, 1:2], gm[:, 1:2], gm[:, 2:3], ALU.subtract).then_inc(s_dv, 1)
            v.wait_ge(s_dv, b * 6 + 6)
            nc.vector.tensor_scalar(gm[:, 1:2], gm[:, 1:2], 0.0, GN_EPS, ALU.max, ALU.add).then_inc(s_gvar, 1)
            v.wait_ge(s_rstd, b + 1)
            nc.vector.scalar_tensor_tensor(gm[:, 3:4], gm[:, 0:1], -1.0, gm[:, 2:3],
                                           ALU.mult, ALU.mult).then_inc(s_norm, 1)

        def gn_tensor(t, b):
            t.wait_ge(s_chan, b + 1)
            nc.tensor.matmul(psum[0:DIM, 7, 448:450], group_avg[:, :], mv[:, :],
                             start=True, stop=True).then_inc(s_grp, 1)

        LN_EXP = "natural_log_exp_and_others"

        def gn_scalar(s, b):
            nc.scalar.preload_act_table_set(LN_EXP)
            s.wait_ge(s_gvar, b + 1)
            nc.scalar.activation(gm[:, 1:2], gm[:, 1:2], ACT.Ln).then_inc(s_lg, 1)
            s.wait_ge(s_lg, b + 1)
            nc.scalar.activation(gm[:, 2:3], gm[:, 1:2], ACT.Exp, scale=-0.5).then_inc(s_rstd, 1)
            s.wait_ge(s_norm, b + 1)

        with ExitStack() as pa:
            def sba(name, shape):
                return pa.enter_context(nc.sbuf_tensor(name, shape, F32))

            def sema(name):
                return pa.enter_context(nc.semaphore(name))

            w_qkv = sba("w_qkv", [DIM, 3 * DIM])
            b_qkv = sba("b_qkv", [DIM, 3])
            w_o = sba("w_o", [DIM, DIM])
            b_o = sba("b_o", [DIM, 1])
            pos_bias = sba("pos_bias", [128, HEADS, TOK])
            xw = sba("xw", [DIM, ROWPIX + 16])
            qT = sba("qT", [DIM, ROWPIX + 16])
            kT = sba("kT", [DIM, ROWPIX])
            v_tok = sba("v_tok", [128, PAIRS, DIM])
            sm = sba("sm", [128, HEADS * PAIRS, 64])
            mx = sba("mx", [128, HEADS * PAIRS])
            rs = sba("rs", [128, HEADS * PAIRS])
            attT = sba("attT", [128, HEADS, 256])
            smt = sm[:, :, 0:TOK]
            oT = sba("oT", [DIM, ROWPIX])
            proj = sba("proj", [DIM, ROWPIX])

            s_xw = sema("s_xw")
            s_qk = sema("s_qk")
            s_v = sema("s_v")
            s_qkev = sema("s_qkev")
            s_vev = sema("s_vev")
            s_score = sema("s_score")
            s_ss = sema("s_ss")
            s_sub = sema("s_sub")
            s_exp = sema("s_exp")
            s_att = sema("s_att")
            s_tr = sema("s_tr")
            s_trev = sema("s_trev")
            s_o = sema("s_o")
            s_oev = sema("s_oev")
            s_pr = sema("s_pr")
            s_prev = sema("s_prev")
            s_res = sema("s_res")
            s_pad = sema("s_pad")

            rings = [s_xw, s_qk, s_v, s_qkev, s_vev, s_score, s_sub, s_exp, s_att, s_tr, s_trev, s_o, s_oev,
                     s_pr, s_prev, s_res]

            def done(eng, sem_, g):
                eng.wait_ge(sem_, g + 2)

            def before(eng, sem_, g):
                eng.wait_ge(sem_, g + 1)

            block = pa.enter_context(nc.Block())
            a_loads = [(w_qkv, "w_qkv"), (b_qkv, "b_qkv"), (w_o, "w_o"), (b_o, "b_o"), (pos_bias, "pos_bias")]
            n_w = 16 * (len(loads) + len(a_loads))

            @block.sync
            def _(sp):
                for ring in rings:
                    sp.sem_inc(ring, 1)
                for t, name in loads + a_loads:
                    sp.dma_start(t[tuple(slice(None) for _ in t.shape)], a[name]).then_inc(s_w, 16)
                for par in range(2):
                    sp.dma_start(image[:, par * PIX:(par + 1) * PIX], a["x"][par]).then_inc(s_load[par], 16)

                def body(i, b, par):
                    done(sp, s_res, b * WIN + WIN - 1)
                    sp.dma_start(a["x1"][b], img(par)).then_inc(s_stored[par], 16)

                def reload(i, par):
                    sp.wait_ge(s_stored[par], i * 16 + 16)
                    sp.dma_start(image[:, par * PIX:(par + 1) * PIX], a["x"][i * 2 + 2 + par]).then_inc(s_load[par], 16)

                if images > 2:
                    with nc.sync.Fori(0, images // 2 - 1) as i:
                        for par in range(2):
                            body(i, i * 2 + par, par)
                            reload(i, par)
                for par in range(2):
                    body(None, images - 2 + par, par)
                for par in range(2):
                    sp.wait_ge(s_stored[par], 16 * (images // 2))

            def rows(par, hh, shape):
                v = img(par).rearrange("p (i r w) -> p i r w", r=WIN, w=SIDE)[:, :, bass.ds(hh, 1), :]
                return v.rearrange("p i r (j w) -> p (r w) i j", w=WIN) if shape == "windows" else \
                    v.rearrange("p i r w -> p (r i) w")

            @block.scalar
            def _(s):
                s.wait_ge(s_w, n_w)
                nc.scalar.activation(a_neg[:, :, :], a_neg[:, :, :], ACT.Exp).then_inc(s_const, 1)

                def front(g, par, hh):
                    before(s, s_v, g)
                    nc.scalar.activation(xw[:, 0:ROWPIX].rearrange("p (w i j) -> p w i j", i=WS, j=WS),
                                         rows(par, hh, "windows"), ACT.Identity,
                                         bias=gm[:, 3:4], scale=gm[:, 2:3]).then_inc(s_xw, 1)
                    done(s, s_qk, g)
                    before(s, s_score, g)
                    nc.scalar.activation(qT[:, 0:ROWPIX], psum[0:DIM, 0, 0:ROWPIX], ACT.Identity, bias=b_qkv[:, 0:1])
                    nc.scalar.activation(kT[:, :], psum[0:DIM, 1, 0:ROWPIX], ACT.Identity,
                                         bias=b_qkv[:, 1:2]).then_inc(s_qkev, 1)

                def softmax(g):
                    done(s, s_sub, g)
                    nc.scalar.activation(smt, smt, ACT.Exp).then_inc(s_exp, 1)

                def back(g):
                    done(s, s_tr, g)
                    nc.scalar.activation(attT[:, :, :], psum[:, 3:6, 0:256], ACT.Copy).then_inc(s_trev, 1)
                    done(s, s_o, g)
                    nc.scalar.activation(oT[:, :].rearrange("p (n o x) -> p o n x", n=2, o=2),
                                         psum[0:DIM, 6:8, 0:ROWPIX // 2].rearrange("p o (n x) -> p o n x", n=2),
                                         ACT.Identity,
                                         bias=b_qkv[:, 2:3]).then_inc(s_oev, 1)
                    done(s, s_pr, g)
                    before(s, s_res, g)
                    nc.scalar.activation(proj[:, :].rearrange("p (i j w) -> p w i j", j=WS, w=WIN),
                                         psum[0:DIM, 7, 0:ROWPIX].rearrange("p (w i j) -> p w i j", i=WS, j=WS),
                                         ACT.Identity, bias=b_o[:, 0:1]).then_inc(s_prev, 1)

                def body(i, b, par):
                    gn_scalar(s, b)
                    front(b * WIN, par, 0)
                    with nc.scalar.Fori(0, WIN - 1) as hh:
                        g = b * WIN + hh
                        softmax(g)
                        front(g + 1, par, hh + 1)
                        back(g)
                    softmax(b * WIN + WIN - 1)
                    back(b * WIN + WIN - 1)

                image_loop(nc.scalar, body)

            @block.tensor
            def _(t):
                t.wait_ge(s_w, n_w)
                t.wait_ge(s_pad, 1)

                def front(g):
                    done(t, s_xw, g)
                    before(t, s_qkev, g)
                    nc.tensor.matmul(psum[0:DIM, 0, 0:ROWPIX], w_qkv[:, 0:DIM], xw[:, 0:ROWPIX], start=True, stop=True)
                    nc.tensor.matmul(psum[0:DIM, 1, 0:ROWPIX], w_qkv[:, DIM:2 * DIM], xw[:, 0:ROWPIX],
                                     start=True, stop=True).then_inc(s_qk, 1)
                    before(t, s_vev, g)
                    for w in range(WIN):
                        base, slot = window(w)
                        mm = nc.tensor.matmul(psum[base:base + 64, 2, slot * DIM:(slot + 1) * DIM],
                                              xw[:, w * TOK:w * TOK + 64],
                                              w_qkv[:, 2 * DIM:3 * DIM], start=True, stop=True)
                    mm.then_inc(s_v, 1)

                def window(w):
                    pair, side = divmod(w, 2)
                    return 64 * (pair % 2), pair // 2 * 2 + side

                def scores(g):
                    done(t, s_qkev, g)
                    before(t, s_trev, g)
                    for w in range(WIN):
                        for h in range(HEADS):
                            r = slice(HEAD_DIM * h, HEAD_DIM * (h + 1))
                            p0, col = 64 * (w % 2), (w // 2) * TOK
                            mm = nc.tensor.matmul(psum[p0:p0 + 64, 3 + h, col:col + TOK],
                                                  qT[r, w * TOK:w * TOK + 64], kT[r, w * TOK:(w + 1) * TOK],
                                                  start=True, stop=True)
                    mm.then_inc(s_score, 1)

                def back(g):
                    done(t, s_att, g)
                    for h in range(HEADS):
                        for p in range(2):
                            two = slice(h * PAIRS + 2 * p, h * PAIRS + 2 * p + 2)
                            mm = nc.tensor.transpose(psum[:, 3 + h, p * 128:(p + 1) * 128],
                                                     sm[:, two, :].rearrange("p t m -> p (t m)"), ident[:, :])
                    mm.then_inc(s_tr, 1)
                    done(t, s_trev, g)
                    done(t, s_vev, g)
                    before(t, s_prev, g)
                    t.sem_inc(s_gate, 1)
                    for w in range(WIN):
                        for h in range(HEADS):
                            base, slot = window(w)
                            mm = nc.tensor.matmul(psum[HEAD_DIM * h:HEAD_DIM * (h + 1), 6 + base // 64,
                                                       slot * TOK:(slot + 1) * TOK],
                                                  v_tok[base:base + TOK, slot, HEAD_DIM * h:HEAD_DIM * (h + 1)],
                                                  attT[base:base + TOK, h, slot * 64:slot * 64 + TOK],
                                                  start=True, stop=True)
                    mm.then_inc(s_o, 1)
                    done(t, s_oev, g)
                    nc.tensor.matmul(psum[0:DIM, 7, 0:ROWPIX], w_o[:, :], oT[:, :],
                                     start=True, stop=True).then_inc(s_pr, 1)

                def body(i, b, par):
                    before(t, s_prev, b * WIN)
                    gn_tensor(t, b)
                    front(b * WIN)
                    with nc.tensor.Fori(0, WIN - 1) as hh:
                        g = b * WIN + hh
                        scores(g)
                        front(g + 1)
                        back(g)
                    scores(b * WIN + WIN - 1)
                    back(b * WIN + WIN - 1)

                image_loop(nc.tensor, body)

            @block.vector
            def _(v):
                nc.vector.memset(qT[:, ROWPIX:], 0.0)
                nc.vector.memset(sm[:, :, :], 0.0)
                nc.vector.memset(xw[:, ROWPIX:], 0.0).then_inc(s_pad, 1)
                nc.vector.memset(eps[:, :], LN_EPS)
                v.wait_ge(s_w, n_w)
                nc.vector.tensor_reduce(d_sum[:, :], d_skip[:, :, :], AX.X, ALU.add).then_inc(s_const, 1)
                v.wait_ge(s_const, 2)
                nc.vector.tensor_scalar(a_neg[:, :, :], a_neg[:, :, :], -1.0, None, ALU.mult).then_inc(s_const, 1)

                def values(g):
                    done(v, s_v, g)
                    before(v, s_o, g)
                    nc.vector.tensor_copy(v_tok[:, :, :].rearrange("p w c -> p (w c)"),
                                          psum[:, 2, 0:4 * DIM]).then_inc(s_vev, 1)

                def softmax_top(g):
                    done(v, s_score, g)
                    before(v, s_tr, g)
                    for h in range(HEADS):
                        st = nc.vector.scalar_tensor_tensor(
                            sm[:, h * PAIRS:(h + 1) * PAIRS, 0:TOK],
                            psum[:, 3 + h, 0:PAIRS * TOK].rearrange("p (w m) -> p w m", m=TOK), SCALE,
                            pos_bias[:, h:h + 1, :].to_broadcast([128, PAIRS, TOK]), ALU.mult, ALU.add)
                    st.then_inc(s_ss, 1)
                    v.wait_ge(s_ss, g * 4 + 1)
                    nc.vector.tensor_reduce(mx[:, :], smt, AX.X, ALU.max).then_inc(s_ss, 1)
                    v.wait_ge(s_ss, g * 4 + 2)
                    nc.vector.tensor_tensor(smt, smt,
                                            mx[:, :].unsqueeze(2).to_broadcast([128, HEADS * PAIRS, TOK]),
                                            ALU.subtract).then_inc(s_sub, 1)

                def softmax_low(g):
                    done(v, s_exp, g)
                    nc.vector.tensor_reduce(mx[:, :], smt, AX.X, ALU.add).then_inc(s_ss, 1)
                    v.wait_ge(s_ss, g * 4 + 3)
                    nc.vector.reciprocal(rs[:, :], mx[:, :]).then_inc(s_ss, 1)
                    v.wait_ge(s_ss, g * 4 + 4)
                    nc.vector.tensor_tensor(smt, smt,
                                            rs[:, :].unsqueeze(2).to_broadcast([128, HEADS * PAIRS, TOK]),
                                            ALU.mult).then_inc(s_att, 1)

                def body(i, b, par):
                    def ready():
                        v.wait_ge(s_load[par], i * 16 + 16)
                        before(v, s_xw, b * WIN)
                    gn_vector(v, b, par, ready)
                    values(b * WIN)
                    with nc.vector.Fori(0, WIN - 1) as hh:
                        g = b * WIN + hh
                        softmax_top(g)
                        softmax_low(g)
                        values(g + 1)
                    softmax_top(b * WIN + WIN - 1)
                    softmax_low(b * WIN + WIN - 1)

                image_loop(nc.vector, body)

            @block.gpsimd
            def _(p):
                def body(i, b, par):
                    with nc.gpsimd.Fori(0, WIN) as hh:
                        g = b * WIN + hh
                        done(p, s_prev, g)
                        r = rows(par, hh, "rows")
                        nc.gpsimd.tensor_tensor(r, r, proj[:, :].rearrange("p (i w) -> p i w", w=SIDE),
                                                ALU.add).then_inc(s_res, 1)

                image_loop(nc.gpsimd, body)

        with ExitStack() as pb:
            def sbb(name, shape, dtype=F32):
                return pb.enter_context(nc.sbuf_tensor(name, shape, dtype))

            def semb(name):
                return pb.enter_context(nc.semaphore(name))

            conv_diag = sbb("conv_diag", [DIM, HALVES, 9, DIM])
            xn = sbb("xn", [DIM, PIX])
            u = sbb("u", [DIM, HALVES, PIX])
            y = sbb("y", [DIM, HALVES, PIX])
            h = sbb("h", [128, TILES, CH])
            xx = h[0:DIM, :, :].rearrange("p t c -> p (t c)")[:, 0:HALVES * PADDED * PADDED].rearrange(
                "p (f r w) -> p f r w", f=HALVES, r=PADDED)
            dbu = sbb("dbu", [128, 2, CH])
            hc = sbb("hc", [128, 3, CH])
            bc = sbb("bc", [128, 2, 8, CH])
            delta = sbb("delta", [DIM, HALVES, 2, CH], F32R)
            du = sbb("du", [DIM, HALVES, 2, CH], F32R)
            xd = sbb("xd", [XD_ROWS, CH])
            xd2 = sbb("xd2", [XD_ROWS, 2, CH], F32R)
            zc = sbb("zc", [DIM, CH])
            ze = sbb("ze", [DIM, CH])
            zl = sbb("zl", [DIM, CH])
            rep_stage = bc[0:DIM, 0, 0, 0:3 * 128]
            bc_stage = bc[0:XD_ROWS, 0, 1:5, :].rearrange("p j c -> p (j c)")[:, 0:8 * 128]
            pair = dbu[0:DIM, :, :]

            def rep_delta(g):
                return psum[:, g % 2, 0:CH]

            def rep_du(g):
                return psum[:, 2 + g % 2, 0:CH]

            def decay(q):
                return psum[:, 4 + q % 2, 0:CH]

            Y_BANK, P_BANK = 6, 7
            LAG = 2

            s_diag = semb("s_diag")
            s_xn = semb("s_xn")
            s_zero = semb("s_zero")
            s_xx = semb("s_xx")
            s_xxev = semb("s_xxev")
            s_cv = semb("s_cv")
            s_u = semb("s_u")
            s_y0 = semb("s_y0")
            s_mean = semb("s_mean")
            s_yc = semb("s_yc")
            s_sq = semb("s_sq")
            s_var = semb("s_var")
            s_lv = semb("s_lv")
            s_rr = semb("s_rr")
            s_nrm = semb("s_nrm")
            s_aff = semb("s_aff")
            s_zz = semb("s_zz")
            s_zev = semb("s_zev")
            s_g = semb("s_g")
            s_op = semb("s_op")
            s_fin = semb("s_fin")
            s_rep = semb("s_rep")
            s_da = semb("s_da")
            s_b = semb("s_b")
            s_h = semb("s_h")
            s_hc = semb("s_hc")
            s_sum = semb("s_sum")
            s_yev = semb("s_yev")
            s_pm = semb("s_pm")
            s_pf = semb("s_pf")
            s_xh = semb("s_xh")
            s_dh = semb("s_dh")
            s_dl = semb("s_dl")
            s_uh = semb("s_uh")
            s_ul = semb("s_ul")
            s_stage = semb("s_stage")
            s_sel = semb("s_sel")
            s_zc = semb("s_zc")
            s_ze = semb("s_ze")
            s_zl = semb("s_zl")
            s_du = semb("s_du")
            starts = [(s_xxev, 2), (s_u, 2), (s_yc, 1), (s_nrm, 1), (s_zev, 1), (s_g, 1), (s_fin, 1),
                      (s_da, 8), (s_b, 8), (s_h, 2), (s_hc, TILES), (s_sum, 3), (s_yev, 1), (s_pf, 1),
                      (s_dl, 1), (s_ul, 1)]

            block = pb.enter_context(nc.Block())

            def chunk_of(t, k, c):
                pos = c if k < 2 else CHUNKS - 1 - c
                if k % 2 == 0:
                    return t[:, bass.ds(pos * CH, CH)].rearrange("p (l s) -> p l s", s=SIDE)
                return t.rearrange("p (h w) -> p w h", w=SIDE)[:, bass.ds(pos * LINES, LINES), :]

            def flat(t):
                return t.rearrange("p (l s) -> p l s", s=SIDE)

            def directed(t, k):
                return t if k < 2 else t[:, ::-1]

            def chunk_loop(eng, b, chunk):
                for k in range(DIRS):
                    base = b * (DIRS * CHUNKS) + k * CHUNKS
                    parity = k * CHUNKS % 2

                    def one(c, back, ahead):
                        chunk(k, c, base + c, (parity + back) % 2, (k, c - 1) if back else before_first,
                              (k, c + 1) if ahead else after_last)

                    before_first = (k - 1, CHUNKS - 1) if k else None
                    after_last = (k + 1, 0) if k + 1 < DIRS else None
                    one(0, 0, True)
                    with eng.Fori(0, (CHUNKS - 3) // 2) as j:
                        one(j * 2 + 1, 1, True)
                        one(j * 2 + 2, 2, True)
                    one(CHUNKS - 2, CHUNKS - 2, True)
                    one(CHUNKS - 1, CHUNKS - 1, False)

            @block.sync
            def _(sp):
                for sem_, n in starts:
                    sp.sem_inc(sem_, n)
                for stage, name in ((rep_stage, "rep_sel"), (bc_stage, "bc_sel")):
                    sp.dma_start(stage, a[name].rearrange("p j m -> p (j m)")).then_inc(s_stage, 16)
                half = images // 2

                def load(par, b, n):
                    sp.wait_ge(s_stored[par], (half + n) * 16)
                    sp.dma_start(image[:, par * PIX:(par + 1) * PIX], a["x1"][b]).then_inc(s_load[par], 16)

                def store(b, par):
                    sp.wait_ge(s_fin, (b + 1) * CHUNKS + 1)
                    sp.dma_start(a["out"][b], img(par)).then_inc(s_stored[par], 16)

                for par in range(2):
                    load(par, par, 0)
                if images > 2:
                    with nc.sync.Fori(0, half - 1) as i:
                        for par in range(2):
                            store(i * 2 + par, par)
                            load(par, i * 2 + 2 + par, i + 1)
                for par in range(2):
                    store(images - 2 + par, par)
                for par in range(2):
                    sp.wait_ge(s_stored[par], 2 * half * 16)

            @block.tensor
            def _(t):
                t.wait_ge(s_sel, 2)
                t.wait_ge(s_diag, 1)

                def item(k, c, P, n):
                    t.wait_ge(s_pf, P * PREPS + n + 1)
                    kind, j, _ = ITEMS[n]
                    out = psum[:, P_BANK, 0:CH]
                    if kind == "proj":
                        for f in range(HALVES):
                            mm = nc.tensor.matmul(flat(out[0:XD_ROWS, :]), xproj[:, k, f, :],
                                                  chunk_of(u[:, f, :], k, c), start=(f == 0), stop=(f == 1))
                    elif kind == "dt":
                        mm = nc.tensor.matmul(out[0:DIM, :], dt_w[:, k, j * DIM:(j + 1) * DIM], xd[:, :],
                                              start=True, stop=True)
                    else:
                        for part in range(2):
                            mm = nc.tensor.matmul(out, bc_sel[:, j, :], xd2[:, part, :],
                                                  start=(part == 0), stop=(part == 1))
                    mm.then_inc(s_pm, 1)

                def replicate(P, g):
                    f, quadrant = g // 3, g % 3
                    t.wait_ge(s_ul, P * HALVES + f + 2)
                    t.wait_ge(s_da, P * TILES + g * QUADS + 4)
                    t.wait_ge(s_b, P * TILES + g * QUADS + 4)
                    for part in range(2):
                        nc.tensor.matmul(rep_delta(g), rep_sel[:, quadrant, :], delta[:, f, part, :],
                                         start=(part == 0), stop=(part == 1))
                    for part in range(2):
                        mm = nc.tensor.matmul(rep_du(g), rep_sel[:, quadrant, :], du[:, f, part, :],
                                              start=(part == 0), stop=(part == 1))
                    mm.then_inc(s_rep, 1)

                def tile_sum(G, q):
                    place = q % (TILES // 2)
                    if place == 0:
                        t.wait_ge(s_yev, G * HALVES + q // (TILES // 2) + 1)
                    t.wait_ge(s_hc, G * TILES + q + 1 + TILES)
                    nc.tensor.matmul(psum[0:DIM, Y_BANK, 0:CH], sum_sel[:, place // QUADS, :], hc[:, q % 3, :],
                                     start=(place == 0), stop=(place == TILES // 2 - 1)).then_inc(s_sum, 1)

                def chunk(k, c, G, par, prev, nxt):
                    for q in range(TILES):
                        if q % QUADS == 0:
                            if q + QUADS < TILES:
                                replicate(G, q // QUADS + 1)
                            elif nxt:
                                replicate(G + 1, 0)
                        for n in range(PREPS):
                            if nxt and q == ITEMS[n][2]:
                                item(*nxt, G + 1, n)
                        if q >= LAG:
                            tile_sum(G, q - LAG)
                        elif prev:
                            tile_sum(G - 1, q - LAG + TILES)
                    if not nxt:
                        for q in range(TILES - LAG, TILES):
                            tile_sum(G, q)

                def body(i, b, par):
                    t.wait_ge(s_pf, b * (DIRS * CHUNKS * PREPS) + 1)
                    gn_tensor(t, b + images)
                    t.wait_ge(s_xn, b + 1)
                    for n in range(2 * CHUNKS):
                        c, f = divmod(n, HALVES)
                        t.wait_ge(s_xxev, b * 14 + n + 1)
                        nc.tensor.matmul(psum[0:DIM, n % 2, 0:CH], w_in[:, f * DIM:(f + 1) * DIM],
                                         xn[:, c * CH:(c + 1) * CH], start=True, stop=True).then_inc(s_xx, 1)
                    t.wait_ge(s_xxev, b * 14 + 14 + 2)
                    for n in range(2 * CHUNKS):
                        c, f = divmod(n, HALVES)
                        t.wait_ge(s_u, b * 14 + n + 1)
                        for tap in range(9):
                            dr, dc = divmod(tap, 3)
                            mm = nc.tensor.matmul(flat(psum[0:DIM, 2 + n % 2, 0:CH]), conv_diag[:, f, tap, :],
                                                  xx[:, f, c * LINES + dr:c * LINES + dr + LINES, dc:dc + SIDE],
                                                  start=(tap == 0), stop=(tap == 8))
                        mm.then_inc(s_cv, 1)
                    t.wait_ge(s_u, b * 14 + 14 + 2)
                    P = b * (DIRS * CHUNKS)
                    for n in range(PREPS):
                        item(0, 0, P, n)
                    replicate(P, 0)
                    chunk_loop(nc.tensor, b, chunk)
                    t.wait_ge(s_yev, (b + 1) * 2 * DIRS * CHUNKS + 1)
                    for c in range(CHUNKS):
                        cs = slice(c * CH, (c + 1) * CH)
                        t.wait_ge(s_yc, b * CHUNKS + c + 1)
                        for f in range(HALVES):
                            mm = nc.tensor.matmul(psum[0:DIM, 0, 0:CH], inner_avg[:, :], y[:, f, cs],
                                                  start=(f == 0), stop=(f == 1))
                        mm.then_inc(s_mean, 1)
                        t.wait_ge(s_sq, b * CHUNKS + c + 1)
                        for f in range(HALVES):
                            mm = nc.tensor.matmul(psum[0:DIM, 1, 0:CH], inner_avg[:, :], pair[:, f, :],
                                                  start=(f == 0), stop=(f == 1))
                        mm.then_inc(s_var, 1)
                    for c in range(CHUNKS):
                        cs = slice(c * CH, (c + 1) * CH)
                        t.wait_ge(s_zev, b * CHUNKS + c + 1)
                        for f in range(HALVES):
                            mm = nc.tensor.matmul(psum[0:DIM, 2 + f, 0:CH],
                                                  w_in[:, INNER + f * DIM:INNER + (f + 1) * DIM], xn[:, cs],
                                                  start=True, stop=True)
                        mm.then_inc(s_zz, 1)
                        t.wait_ge(s_g, b * CHUNKS + c + 2)
                        t.wait_ge(s_fin, b * CHUNKS + c + 1)
                        for f in range(HALVES):
                            mm = nc.tensor.matmul(psum[0:DIM, 4, 0:CH], w_out2[:, f, :], y[:, f, cs],
                                                  start=(f == 0), stop=(f == 1))
                        mm.then_inc(s_op, 1)

                image_loop(nc.tensor, body)

            @block.scalar
            def _(s):
                s.wait_ge(s_const, 3)
                s.wait_ge(s_stage, 32)
                nc.scalar.activation(rep_sel[:, :, :].rearrange("p j m -> p (j m)"), rep_stage, ACT.Copy).then_inc(s_sel, 1)
                nc.scalar.activation(bc_sel[:, :, :].rearrange("p j m -> p (j m)"), bc_stage, ACT.Copy).then_inc(s_sel, 1)

                def take(P, par, n):
                    s.wait_ge(s_pm, P * PREPS + n + 1)
                    kind, j, _ = ITEMS[n]
                    src = psum[:, P_BANK, 0:CH]
                    if kind == "proj":
                        nc.scalar.activation(xd[:, :], src[0:XD_ROWS, :], ACT.Copy)
                        nc.scalar.activation(xd2[:, 0, :], src[0:XD_ROWS, :], ACT.Copy).then_inc(s_xh, 1)
                    else:
                        nc.scalar.activation(bc[:, par, j, :], src, ACT.Copy).then_inc(s_pf, 1)

                def softplus(P, f):
                    s.wait_ge(s_zc, P * HALVES + f + 1)
                    s.wait_ge(s_ul, P * HALVES + f + 1)
                    nc.scalar.activation(ze[:, :], zc[:, :], ACT.Exp).then_inc(s_ze, 1)
                    s.wait_ge(s_ze, P * HALVES + f + 1)
                    nc.scalar.activation(zl[:, :], ze[:, :], ACT.Ln, bias=1.0).then_inc(s_zl, 1)

                def delta_high(P, f):
                    s.wait_ge(s_pf, P * PREPS + DT_ITEM[f] + 2)
                    nc.scalar.activation(delta[:, f, 0, :], zc[:, :], ACT.Copy).then_inc(s_dh, 1)

                def du_high(P, f):
                    s.wait_ge(s_du, P * HALVES + f + 1)
                    nc.scalar.activation(du[:, f, 0, :], ze[:, :], ACT.Copy).then_inc(s_uh, 1)

                def chunk(k, c, G, par, prev, nxt):
                    for q in range(TILES):
                        g = q // QUADS
                        s.wait_ge(s_rep, G * DGROUPS + g + 1)
                        s.wait_ge(s_h, G * TILES + q + 1)
                        nc.scalar.activation(decay(q), rep_delta(g), ACT.Exp,
                                             scale=a_neg[:, k, q:q + 1]).then_inc(s_da, 1)
                        if not nxt:
                            continue
                        for f in range(HALVES):
                            if q - 2 == DT_SLOT[f]:
                                softplus(G + 1, f)
                            if q == HIGH_SLOT[f]:
                                s.wait_ge(s_rep, G * DGROUPS + 3 * f + 3)
                                delta_high(G + 1, f)
                            if q == HIGH_SLOT[f] + 1:
                                du_high(G + 1, f)
                        for n in range(PREPS):
                            if ITEMS[n][0] != "dt" and q - 1 == ITEMS[n][2]:
                                if n == 2:
                                    s.wait_ge(s_hc, (G + 1) * TILES)
                                take(G + 1, 1 - par, n)

                def body(i, b, par):
                    gn_scalar(s, b + images)
                    nc.scalar.activation(xn[:, :], img(par), ACT.Identity, bias=gm[:, 3:4],
                                         scale=gm[:, 2:3]).then_inc(s_xn, 1)
                    s.wait_ge(s_zero, b + 1)
                    for n in range(2 * CHUNKS):
                        c, f = divmod(n, HALVES)
                        s.wait_ge(s_xx, b * 14 + n + 1)
                        nc.scalar.activation(xx[:, f, 1 + c * LINES:1 + (c + 1) * LINES, 1:1 + SIDE],
                                             flat(psum[0:DIM, n % 2, 0:CH]), ACT.Copy).then_inc(s_xxev, 1)
                    for n in range(2 * CHUNKS):
                        c, f = divmod(n, HALVES)
                        s.wait_ge(s_cv, b * 14 + n + 1)
                        nc.scalar.activation(u[:, f, c * CH:(c + 1) * CH], psum[0:DIM, 2 + n % 2, 0:CH],
                                             ACT.Silu, bias=conv_b[:, f:f + 1]).then_inc(s_u, 1)
                    nc.scalar.preload_act_table_set(LN_EXP)
                    P = b * (DIRS * CHUNKS)
                    for n in range(PREPS):
                        if ITEMS[n][0] == "dt":
                            softplus(P, ITEMS[n][1])
                            delta_high(P, ITEMS[n][1])
                            du_high(P, ITEMS[n][1])
                        else:
                            take(P, 0, n)
                    chunk_loop(nc.scalar, b, chunk)
                    for c in range(CHUNKS):
                        cs = slice(c * CH, (c + 1) * CH)
                        s.wait_ge(s_yc, b * CHUNKS + c + 2)
                        nc.scalar.activation(pair[:, :, :], y[:, :, cs], ACT.Square).then_inc(s_sq, 1)
                        s.wait_ge(s_var, b * CHUNKS + c + 1)
                        nc.scalar.activation(ze[:, :], psum[0:DIM, 1, 0:CH], ACT.Ln, bias=eps[0:DIM, :]).then_inc(s_lv, 1)
                        s.wait_ge(s_lv, b * CHUNKS + c + 1)
                        s.wait_ge(s_nrm, b * CHUNKS + c + 1)
                        nc.scalar.activation(zl[:, :], ze[:, :], ACT.Exp, scale=-0.5).then_inc(s_rr, 1)
                    for c in range(CHUNKS):
                        s.wait_ge(s_zz, b * CHUNKS + c + 1)
                        s.wait_ge(s_g, b * CHUNKS + c + 1)
                        nc.scalar.activation(pair[:, :, :], psum[0:DIM, 2:4, 0:CH], ACT.Silu).then_inc(s_zev, 1)

                image_loop(nc.scalar, body)

            @block.vector
            def _(v):
                for f in range(HALVES):
                    for tap in range(9):
                        ins = nc.vector.tensor_scalar(conv_diag[:, f, tap, :], ident[0:DIM, 0:DIM],
                                                      conv_w[:, f, tap:tap + 1], None, ALU.mult)
                ins.then_inc(s_diag, 1)
                v.wait_ge(s_const, 3)

                def xd_low(P):
                    v.wait_ge(s_xh, P + 1)
                    nc.vector.tensor_tensor(xd2[:, 1, :], psum[0:XD_ROWS, P_BANK, 0:CH],
                                            xd2[:, 0, :].bitcast(F32), ALU.subtract).then_inc(s_pf, 1)

                def argument(k, P, f):
                    v.wait_ge(s_pm, P * PREPS + DT_ITEM[f] + 1)
                    v.wait_ge(s_dl, P * HALVES + f + 1)
                    nc.vector.tensor_scalar(zc[:, :], psum[0:DIM, P_BANK, 0:CH], dt_b[:, k, f:f + 1], SOFTPLUS_TOP,
                                            ALU.add, ALU.min).then_inc(s_zc, 1)

                def make_delta(k, P, f):
                    v.wait_ge(s_zl, P * HALVES + f + 1)
                    nc.vector.scalar_tensor_tensor(zc[:, :], psum[0:DIM, P_BANK, 0:CH], dt_b[:, k, f:f + 1],
                                                   zl[:, :], ALU.add, ALU.max).then_inc(s_pf, 1)

                def times_b(G, par, q):
                    g, j = divmod(q, QUADS)
                    if q == 0:
                        v.wait_ge(s_pf, G * PREPS + PREPS + 1)
                    v.wait_ge(s_rep, G * DGROUPS + g + 1)
                    v.wait_ge(s_h, G * TILES + q + 1)
                    nc.vector.tensor_tensor(dbu[:, q % 2, :], rep_du(g), bc[:, par, j, :], ALU.mult).then_inc(s_b, 1)

                def add_half(k, c, G, f):
                    yk = chunk_of(y[:, f, :], k, c)
                    v.wait_ge(s_sum, G * TILES + (f + 1) * TILES // 2 + 3)
                    v.sem_inc(s_gate, 1)
                    nc.vector.tensor_tensor(yk, flat(psum[0:DIM, Y_BANK, 0:CH]), yk, ALU.add).then_inc(s_yev, 1)

                def chunk(k, c, G, par, prev, nxt):
                    edge = CH - 1 if k < 2 else 0
                    for q in range(TILES):
                        if q + 1 < TILES:
                            times_b(G, par, q + 1)
                        elif nxt:
                            times_b(G + 1, 1 - par, 0)
                        v.wait_ge(s_da, G * TILES + q + 1 + 8)
                        v.wait_ge(s_b, G * TILES + q + 1 + 8)
                        v.wait_ge(s_hc, G * TILES + q + 1)
                        nc.vector.tensor_tensor_scan(directed(h[:, q, :], k), directed(decay(q), k),
                                                     directed(dbu[:, q % 2, :], k),
                                                     0.0 if isinstance(c, int) and c == 0 else h[:, q, edge:edge + 1],
                                                     ALU.mult, ALU.add).then_inc(s_h, 1)
                        if nxt:
                            for f in range(HALVES):
                                if q - 1 == DT_SLOT[f]:
                                    argument(nxt[0], G + 1, f)
                                if q - 3 == DT_SLOT[f]:
                                    make_delta(nxt[0], G + 1, f)
                            if q - 2 == ITEMS[0][2]:
                                xd_low(G + 1)
                        if q == TILES // 2 + LAG + 1:
                            add_half(k, c, G, 0)
                        if q == LAG + 1 and prev:
                            add_half(*prev, G - 1, 1)
                    if not nxt:
                        add_half(k, c, G, 1)

                def body(i, b, par):
                    half = images // 2

                    def ready():
                        v.wait_ge(s_load[par], (half + 1 + i) * 16)
                    gn_vector(v, b + images, par, ready)
                    v.wait_ge(s_u, b * 14 + 14 + 2)
                    for f in range(HALVES):
                        ins = nc.vector.tensor_scalar(y[:, f, :], u[:, f, :], d_sum[:, f:f + 1], None, ALU.mult)
                    ins.then_inc(s_y0, 1)
                    P = b * (DIRS * CHUNKS)
                    xd_low(P)
                    for f in range(HALVES):
                        argument(0, P, f)
                        make_delta(0, P, f)
                    v.wait_ge(s_y0, b + 1)
                    times_b(P, 0, 0)
                    chunk_loop(nc.vector, b, chunk)
                    for c in range(CHUNKS):
                        cs = slice(c * CH, (c + 1) * CH)
                        v.wait_ge(s_mean, b * CHUNKS + c + 1)
                        for f in range(HALVES):
                            ins = nc.vector.tensor_tensor(y[:, f, cs], y[:, f, cs], psum[0:DIM, 0, 0:CH], ALU.subtract)
                        ins.then_inc(s_yc, 1)
                        if c:
                            affine(b, c - 1)
                    affine(b, CHUNKS - 1)
                    for c in range(CHUNKS):
                        v.wait_ge(s_op, b * CHUNKS + c + 1)
                        x = img(par)[:, c * CH:(c + 1) * CH]
                        nc.vector.tensor_tensor(x, psum[0:DIM, 4, 0:CH], x, ALU.add).then_inc(s_fin, 1)

                def affine(b, c):
                    v.wait_ge(s_nrm, b * CHUNKS + c + 2)
                    for f in range(HALVES):
                        yf = y[:, f, c * CH:(c + 1) * CH]
                        ins = nc.vector.tensor_scalar(yf, yf, ln_w[:, f:f + 1], ln_b[:, f:f + 1], ALU.mult, ALU.add)
                    ins.then_inc(s_aff, 1)

                image_loop(nc.vector, body)

            @block.gpsimd
            def _(p):
                def make_du(k, c, P, f):
                    p.wait_ge(s_pf, P * PREPS + DT_ITEM[f] + 2)
                    nc.gpsimd.tensor_tensor(flat(ze[:, :]), flat(zc[:, :]), chunk_of(u[:, f, :], k, c),
                                            ALU.mult).then_inc(s_du, 1)

                def delta_low(P, f):
                    p.wait_ge(s_dh, P * HALVES + f + 1)
                    nc.gpsimd.tensor_tensor(delta[:, f, 1, :], zc[:, :], delta[:, f, 0, :].bitcast(F32),
                                            ALU.subtract).then_inc(s_dl, 1)

                def du_low(P, f):
                    p.wait_ge(s_uh, P * HALVES + f + 1)
                    nc.gpsimd.tensor_tensor(du[:, f, 1, :], ze[:, :], du[:, f, 0, :].bitcast(F32),
                                            ALU.subtract).then_inc(s_ul, 1)

                def chunk(k, c, G, par, prev, nxt):
                    p.wait_ge(s_pf, G * PREPS + PREPS + 1)
                    for q in range(TILES):
                        p.wait_ge(s_h, G * TILES + q + 1 + 2)
                        p.wait_ge(s_sum, G * TILES + q + 1)
                        nc.gpsimd.tensor_tensor(hc[:, q % 3, :], h[:, q, :], bc[:, par, 4 + q % QUADS, :],
                                                ALU.mult).then_inc(s_hc, 1)
                        if nxt:
                            for f in range(HALVES):
                                if q - 4 == DT_SLOT[f]:
                                    make_du(*nxt, G + 1, f)
                                if q - 1 == HIGH_SLOT[f]:
                                    delta_low(G + 1, f)
                                if q - 2 == HIGH_SLOT[f]:
                                    du_low(G + 1, f)

                def body(i, b, par):
                    nc.gpsimd.memset(xx, 0.0).then_inc(s_zero, 1)
                    P = b * (DIRS * CHUNKS)
                    for f in range(HALVES):
                        make_du(0, 0, P, f)
                        delta_low(P, f)
                        du_low(P, f)
                    chunk_loop(nc.gpsimd, b, chunk)
                    for c in range(CHUNKS):
                        cs = slice(c * CH, (c + 1) * CH)
                        p.wait_ge(s_rr, b * CHUNKS + c + 1)
                        nc.gpsimd.tensor_tensor(y[:, :, cs], y[:, :, cs],
                                                zl[:, :].unsqueeze(1).to_broadcast([DIM, HALVES, CH]),
                                                ALU.mult).then_inc(s_nrm, 1)
                    for c in range(CHUNKS):
                        cs = slice(c * CH, (c + 1) * CH)
                        p.wait_ge(s_aff, b * CHUNKS + c + 1)
                        p.wait_ge(s_zev, b * CHUNKS + c + 2)
                        nc.gpsimd.tensor_tensor(y[:, :, cs], y[:, :, cs], pair[:, :, :], ALU.mult).then_inc(s_g, 1)

                image_loop(nc.gpsimd, body)


def selectors():
    rep = np.zeros((DIM, 3, 128), np.float32)
    bc = np.zeros((XD_ROWS, 8, 128), np.float32)
    total = np.zeros((128, 3, DIM), np.float32)
    for m in range(128):
        for quadrant in range(3):
            rep[32 * quadrant + m % 32, quadrant, m] = 1
        for j in range(4):
            bc[B_ROW + 4 * j + m // 32, j, m] = 1
            bc[C_ROW + 4 * j + m // 32, 4 + j, m] = 1
        for quadrant in range(3):
            total[m, quadrant, 32 * quadrant + m % 32] = 1
    groups = np.arange(DIM) // GROUP
    return {"rep_sel": rep, "bc_sel": bc, "sum_sel": total, "ident": np.eye(128, dtype=np.float32),
            "group_avg": (groups[:, None] == groups[None, :]).astype(np.float32) / np.float32(GROUP),
            "inner_avg": np.full((DIM, DIM), 1 / INNER, np.float32)}


def position_index():
    i, j = np.divmod(np.arange(TOK), WS)
    return (i[:, None] - i[None, :] + WS - 1) * (2 * WS - 1) + j[:, None] - j[None, :] + WS - 1


def layouts(inputs):
    g = {k: np.asarray(v) for k, v in inputs.items()}
    images = g["x"].shape[0]

    def halves(v):
        return v.reshape(HALVES, DIM).T

    bias = np.zeros((2, 64, HEADS, TOK), np.float32)
    bias[:, :TOK] = g["L0_conv_rel_pos"][:, position_index()].transpose(1, 0, 2)
    xproj = np.zeros((DIM, DIRS, HALVES, XD_ROWS), np.float32)
    w = g["L1_conv_x_proj_weight"].reshape(DIRS, RANK + 2 * STATE, HALVES, DIM).transpose(3, 0, 2, 1)
    xproj[..., 0:RANK] = w[..., 0:RANK]
    xproj[..., B_ROW:B_ROW + STATE] = w[..., RANK:RANK + STATE]
    xproj[..., C_ROW:C_ROW + STATE] = w[..., RANK + STATE:]
    dt_w = np.zeros((XD_ROWS, DIRS, INNER), np.float32)
    dt_w[0:RANK] = g["L1_conv_dt_projs_weight"].transpose(2, 0, 1)
    a_log = g["L1_conv_A_logs"].reshape(DIRS, DGROUPS, 32, QUADS, 4).transpose(4, 2, 0, 1, 3)
    return selectors() | {
        "x": g["x"].reshape(images, PIX, DIM).transpose(0, 2, 1),
        "w_qkv": g["L0_conv_w_qkv"], "b_qkv": g["L0_conv_b_qkv"].reshape(3, DIM).T,
        "w_o": g["L0_conv_w_out"], "b_o": g["L0_conv_b_out"].reshape(DIM, 1),
        "pos_bias": bias.reshape(128, HEADS, TOK),
        "w_in": g["L1_conv_in_proj_w"].T,
        "conv_w": g["L1_conv_conv_w"].reshape(HALVES, DIM, 9).transpose(1, 0, 2),
        "conv_b": halves(g["L1_conv_conv_b"]),
        "xproj": xproj,
        "dt_w": dt_w,
        "dt_b": g["L1_conv_dt_projs_bias"].reshape(DIRS, HALVES, DIM).transpose(2, 0, 1),
        "a_log": a_log.reshape(128, DIRS, TILES),
        "d_skip": g["L1_conv_Ds"].reshape(DIRS, HALVES, DIM).transpose(2, 1, 0),
        "ln_w": halves(g["L1_conv_ln_w"]), "ln_b": halves(g["L1_conv_ln_b"]),
        "w_out2": g["L1_conv_out_proj_w"].reshape(DIM, HALVES, DIM).transpose(2, 1, 0),
    }


def program(nc, arrays, images):
    a = {n: nc.dram_tensor(f"in_{n}", v.shape, F32, kind="ExternalInput").ap() for n, v in arrays.items()}
    a["x1"] = nc.dram_tensor("x1", (images, DIM, PIX), F32, kind="Internal").ap()
    a["out"] = nc.dram_tensor("out", (images, DIM, PIX), F32, kind="ExternalOutput").ap()
    build(nc, a, images)


def kernel(**inputs):
    from concourse import bacc
    from concourse.bass_utils import run_bass_kernel_spmd

    arrays = {n: np.ascontiguousarray(v) for n, v in layouts(inputs).items()}
    images = arrays["x"].shape[0]
    nc = bacc.Bacc("TRN2", target_bir_lowering=False, num_devices=1, dynamic_dma_scratch_size=1024)
    program(nc, arrays, images)
    r = run_bass_kernel_spmd(nc, [{f"in_{n}": v for n, v in arrays.items()}], core_ids=[0])
    out = r.results[0]["out"]
    return np.ascontiguousarray(out.transpose(0, 2, 1)).reshape(images, SIDE, SIDE, DIM)
```

```python
from contextlib import ExitStack

import numpy as np
import concourse.bass as bass
from concourse import mybir

F32 = mybir.dt.float32
F32R = mybir.dt.float32r
ALU = mybir.AluOpType
ACT = mybir.ActivationFunctionType
AX = mybir.AxisListType

IMAGES, SIDE, DIM = 64, 56, 96
PIX = SIDE * SIDE
GROUP = 3
WS, HEADS = 7, 3
HEAD_DIM = DIM // HEADS
WIN = SIDE // WS
TOK = WS * WS
ROWPIX = WIN * TOK
PAIRS = WIN // 2
SCALE = HEAD_DIM ** (-0.5)
INNER, STATE, RANK, DIRS = 192, 16, 6, 4
HALVES = INNER // DIM
CH = 448
CHUNKS = PIX // CH
LINES = CH // SIDE
DGROUPS = INNER // 32
QUADS = STATE // 4
TILES = DGROUPS * QUADS
GN_EPS = LN_EPS = 1e-5
PADDED = SIDE + 2
B_ROW, C_ROW, XD_ROWS = 32, 64, 80
ONE_ROW = 31

PROJ_SLOT = 3
PROJ_TAKE, PROJ_LOW = 5, 3
DT_SLOT = [6, 14]
SOFTPLUS, DELTA, DU = 2, 1, 2
HIGH, LOW = 8, 3
SPREAD = [(0, 7), (4, 8), (1, 10), (5, 12), (2, 13), (6, 16), (3, 17), (7, 20)]
SPREAD_TAKE = 2
SPREADS = len(SPREAD)
HCS = 8


def build(nc, a, images):
    with ExitStack() as ctx:
        def sb(name, shape, dtype=F32):
            return ctx.enter_context(nc.sbuf_tensor(name, shape, dtype))

        def sem(name):
            return ctx.enter_context(nc.semaphore(name))

        rep_sel = sb("rep_sel", [DIM, 3, 128], F32R)
        bc_sel = sb("bc_sel", [XD_ROWS, 8, 128], F32R)
        sum_sel = sb("sum_sel", [128, 3, DIM])
        ident = sb("ident", [128, 128])
        group_avg = sb("group_avg", [DIM, DIM])
        inner_avg = sb("inner_avg", [DIM, DIM])
        w_in = sb("w_in", [DIM, 2 * INNER])
        conv_w = sb("conv_w", [DIM, HALVES, 9])
        conv_b = sb("conv_b", [DIM, HALVES])
        xproj = sb("xproj", [DIM, DIRS, HALVES, XD_ROWS])
        dt_w = sb("dt_w", [XD_ROWS, DIRS, INNER])
        one_row = sb("one_row", [XD_ROWS, 1])
        a_neg = sb("a_neg", [128, DIRS, TILES])
        d_skip = sb("d_skip", [DIM, HALVES, DIRS])
        d_sum = sb("d_sum", [DIM, HALVES])
        ln_w = sb("ln_w", [DIM, HALVES])
        ln_b = sb("ln_b", [DIM, HALVES])
        w_out2 = sb("w_out2", [DIM, HALVES, DIM])
        eps = sb("eps", [128, 1])
        stats = sb("stats", [DIM, CHUNKS, 6])
        mv = sb("mv", [DIM, 2])
        gm = sb("gm", [DIM, 4])
        image = sb("image", [DIM, 2 * PIX])
        psum = ctx.enter_context(nc.psum_tensor("psum", [128, 8, 512], F32))

        s_w = sem("s_w")
        s_const = sem("s_const")
        s_load = [sem("s_load0"), sem("s_load1")]
        s_stored = [sem("s_stored0"), sem("s_stored1")]
        s_gate = sem("s_gate")

        loads = [(sum_sel, "sum_sel"), (ident, "ident"),
                 (group_avg, "group_avg"), (inner_avg, "inner_avg"), (w_in, "w_in"), (conv_w, "conv_w"),
                 (conv_b, "conv_b"), (xproj, "xproj"), (dt_w, "dt_w"), (one_row, "one_row"), (a_neg, "a_log"),
                 (d_skip, "d_skip"), (ln_w, "ln_w"), (ln_b, "ln_b"), (w_out2, "w_out2")]

        def img(par):
            return image[:, bass.ds(par * PIX, PIX)]

        def image_loop(eng, body):
            with eng.Fori(0, images // 2) as i:
                for par in range(2):
                    body(i, i * 2 + par, par)

        s_chan = sem("s_chan")
        s_grp = sem("s_grp")
        s_gvar = sem("s_gvar")
        s_rstd = sem("s_rstd")
        s_norm = sem("s_norm")
        s_dv = sem("s_dv")
        s_lg = sem("s_lg")

        def gn_vector(v, b, par, ready):
            ready()
            for c in range(CHUNKS):
                ins = nc.vector.bn_stats(stats[:, c, :], img(par)[:, c * CH:(c + 1) * CH])
            ins.then_inc(s_dv, 1)
            v.wait_ge(s_dv, b * 6 + 1)
            v.sem_inc(s_gate, 1)
            nc.vector.bn_aggr(mv[:, :], stats[:, :, :].rearrange("p c s -> p (c s)")).then_inc(s_dv, 1)
            v.wait_ge(s_dv, b * 6 + 2)
            nc.vector.tensor_tensor(gm[:, 0:1], mv[:, 0:1], mv[:, 0:1], ALU.mult).then_inc(s_dv, 1)
            v.wait_ge(s_dv, b * 6 + 3)
            nc.vector.tensor_tensor(mv[:, 1:2], mv[:, 1:2], gm[:, 0:1], ALU.add).then_inc(s_chan, 1)
            v.wait_ge(s_grp, b + 1)
            nc.vector.tensor_copy(gm[:, 0:2], psum[0:DIM, 7, 448:450]).then_inc(s_dv, 1)
            v.wait_ge(s_dv, b * 6 + 4)
            nc.vector.tensor_tensor(gm[:, 2:3], gm[:, 0:1], gm[:, 0:1], ALU.mult).then_inc(s_dv, 1)
            v.wait_ge(s_dv, b * 6 + 5)
            nc.vector.tensor_tensor(gm[:, 1:2], gm[:, 1:2], gm[:, 2:3], ALU.subtract).then_inc(s_dv, 1)
            v.wait_ge(s_dv, b * 6 + 6)
            nc.vector.tensor_scalar(gm[:, 1:2], gm[:, 1:2], 0.0, GN_EPS, ALU.max, ALU.add).then_inc(s_gvar, 1)
            v.wait_ge(s_rstd, b + 1)
            nc.vector.scalar_tensor_tensor(gm[:, 3:4], gm[:, 0:1], -1.0, gm[:, 2:3],
                                           ALU.mult, ALU.mult).then_inc(s_norm, 1)

        def gn_tensor(t, b):
            t.wait_ge(s_chan, b + 1)
            nc.tensor.matmul(psum[0:DIM, 7, 448:450], group_avg[:, :], mv[:, :],
                             start=True, stop=True).then_inc(s_grp, 1)

        LN_EXP = "natural_log_exp_and_others"

        def gn_scalar(s, b):
            nc.scalar.preload_act_table_set(LN_EXP)
            s.wait_ge(s_gvar, b + 1)
            nc.scalar.activation(gm[:, 1:2], gm[:, 1:2], ACT.Ln).then_inc(s_lg, 1)
            s.wait_ge(s_lg, b + 1)
            nc.scalar.activation(gm[:, 2:3], gm[:, 1:2], ACT.Exp, scale=-0.5).then_inc(s_rstd, 1)
            s.wait_ge(s_norm, b + 1)

        with ExitStack() as pa:
            def sba(name, shape):
                return pa.enter_context(nc.sbuf_tensor(name, shape, F32))

            def sema(name):
                return pa.enter_context(nc.semaphore(name))

            w_qkv = sba("w_qkv", [DIM, 3 * DIM])
            b_qkv = sba("b_qkv", [DIM, 3])
            w_o = sba("w_o", [DIM, DIM])
            b_o = sba("b_o", [DIM, 1])
            pos_bias = sba("pos_bias", [128, HEADS, TOK])
            xw = sba("xw", [DIM, ROWPIX + 16])
            qT = sba("qT", [DIM, ROWPIX + 16])
            kT = sba("kT", [DIM, ROWPIX])
            v_tok = sba("v_tok", [128, 2, PAIRS, DIM])
            sm = sba("sm", [128, 2, HEADS * PAIRS, 64])
            mx = sba("mx", [128, HEADS * PAIRS])
            rs = sba("rs", [128, HEADS * PAIRS])
            attT = sba("attT", [128, HEADS * 256])
            smt = [sm[:, side, :, 0:TOK] for side in range(2)]
            oT = sba("oT", [DIM, ROWPIX])
            proj = sba("proj", [DIM, ROWPIX])

            s_xw = sema("s_xw")
            s_qk = sema("s_qk")
            s_v = sema("s_v")
            s_qkev = sema("s_qkev")
            s_vev = sema("s_vev")
            s_score = sema("s_score")
            s_ss = sema("s_ss")
            s_sub = sema("s_sub")
            s_exp = sema("s_exp")
            s_att = sema("s_att")
            s_tr = sema("s_tr")
            s_trev = sema("s_trev")
            s_o = sema("s_o")
            s_oev = sema("s_oev")
            s_pr = sema("s_pr")
            s_prev = sema("s_prev")
            s_res = sema("s_res")
            s_pad = sema("s_pad")

            two_buffers = [s_tr, s_o]
            rings = [s_xw, s_qk, s_v, s_qkev, s_vev, s_score, s_sub, s_exp, s_att, s_trev, s_oev, s_pr, s_prev, s_res]

            def done(eng, sem_, g):
                eng.wait_ge(sem_, g + (3 if sem_ in two_buffers else 2))

            def before(eng, sem_, g):
                eng.wait_ge(sem_, g + 1)

            def row_loop(eng, b, first, step):
                first(b * WIN)
                with eng.Fori(0, (WIN - 2) // 2) as j:
                    for side in range(2):
                        step(b * WIN + j * 2 + side, side, j * 2 + side + 2, True)
                step(b * WIN + WIN - 2, 0, None, True)
                step(b * WIN + WIN - 1, 1, None, False)

            block = pa.enter_context(nc.Block())
            a_loads = [(w_qkv, "w_qkv"), (b_qkv, "b_qkv"), (w_o, "w_o"), (b_o, "b_o"), (pos_bias, "pos_bias")]
            n_w = 16 * (len(loads) + len(a_loads))

            @block.sync
            def _(sp):
                for ring in rings:
                    sp.sem_inc(ring, 1)
                for ring in two_buffers:
                    sp.sem_inc(ring, 2)
                for t, name in loads + a_loads:
                    sp.dma_start(t[tuple(slice(None) for _ in t.shape)], a[name]).then_inc(s_w, 16)
                for par in range(2):
                    sp.dma_start(image[:, par * PIX:(par + 1) * PIX], a["x"][par]).then_inc(s_load[par], 16)

                def body(i, b, par):
                    done(sp, s_res, b * WIN + WIN - 1)
                    sp.dma_start(a["x1"][b], img(par)).then_inc(s_stored[par], 16)

                def reload(i, par):
                    sp.wait_ge(s_stored[par], i * 16 + 16)
                    sp.dma_start(image[:, par * PIX:(par + 1) * PIX], a["x"][i * 2 + 2 + par]).then_inc(s_load[par], 16)

                if images > 2:
                    with nc.sync.Fori(0, images // 2 - 1) as i:
                        for par in range(2):
                            body(i, i * 2 + par, par)
                            reload(i, par)
                for par in range(2):
                    body(None, images - 2 + par, par)
                for par in range(2):
                    sp.wait_ge(s_stored[par], 16 * (images // 2))

            def rows(par, hh, shape):
                v = img(par).rearrange("p (i r w) -> p i r w", r=WIN, w=SIDE)[:, :, bass.ds(hh, 1), :]
                return v.rearrange("p i r (j w) -> p (r w) i j", w=WIN) if shape == "windows" else \
                    v.rearrange("p i r w -> p (r i) w")

            @block.scalar
            def _(s):
                s.wait_ge(s_w, n_w)
                nc.scalar.activation(a_neg[:, :, :], a_neg[:, :, :], ACT.Exp).then_inc(s_const, 1)

                def normalise(g, par, hh):
                    before(s, s_v, g)
                    before(s, s_qk, g)
                    nc.scalar.activation(xw[:, 0:ROWPIX].rearrange("p (w i j) -> p w i j", i=WS, j=WS),
                                         rows(par, hh, "windows"), ACT.Identity,
                                         bias=gm[:, 3:4], scale=gm[:, 2:3]).then_inc(s_xw, 1)

                def take_qk(g):
                    done(s, s_qk, g)
                    before(s, s_score, g)
                    nc.scalar.activation(qT[:, 0:ROWPIX], psum[0:DIM, 0, 0:ROWPIX], ACT.Identity, bias=b_qkv[:, 0:1])
                    nc.scalar.activation(kT[:, :], psum[0:DIM, 1, 0:ROWPIX], ACT.Identity,
                                         bias=b_qkv[:, 1:2]).then_inc(s_qkev, 1)

                def softmax(g, side):
                    done(s, s_sub, g)
                    nc.scalar.activation(smt[side], smt[side], ACT.Exp).then_inc(s_exp, 1)

                def body(i, b, par):
                    def first(g):
                        normalise(g, par, 0)
                        take_qk(g)
                        normalise(g + 1, par, 1)
                        softmax(g, 0)
                        take_qk(g + 1)

                    def step(g, side, row, ahead):
                        if row is not None:
                            normalise(g + 2, par, row)
                        done(s, s_tr, g)
                        nc.scalar.activation(attT[:, :], psum[:, 0:2, :].rearrange("p b c -> p (b c)")[:, 0:6 * 128],
                                             ACT.Copy).then_inc(s_trev, 1)
                        if ahead:
                            softmax(g + 1, 1 - side)
                        done(s, s_o, g)
                        nc.scalar.activation(oT[:, :].rearrange("p (n o x) -> p o n x", n=2, o=2),
                                             psum[0:DIM, 6:8, 0:ROWPIX // 2].rearrange("p o (n x) -> p o n x", n=2),
                                             ACT.Identity, bias=b_qkv[:, 2:3]).then_inc(s_oev, 1)
                        if row is not None:
                            take_qk(g + 2)
                        done(s, s_pr, g)
                        before(s, s_res, g)
                        nc.scalar.activation(proj[:, :].rearrange("p (i j w) -> p w i j", j=WS, w=WIN),
                                             psum[0:DIM, 7, 0:ROWPIX].rearrange("p (w i j) -> p w i j", i=WS, j=WS),
                                             ACT.Identity, bias=b_o[:, 0:1]).then_inc(s_prev, 1)

                    gn_scalar(s, b)
                    row_loop(nc.scalar, b, first, step)

                image_loop(nc.scalar, body)

            @block.tensor
            def _(t):
                t.wait_ge(s_w, n_w)
                t.wait_ge(s_pad, 1)

                def window(w):
                    pair, side = divmod(w, 2)
                    return 64 * (pair % 2), pair // 2 * 2 + side

                def front_qk(g):
                    done(t, s_xw, g)
                    before(t, s_qkev, g)
                    nc.tensor.matmul(psum[0:DIM, 0, 0:ROWPIX], w_qkv[:, 0:DIM], xw[:, 0:ROWPIX], start=True, stop=True)
                    nc.tensor.matmul(psum[0:DIM, 1, 0:ROWPIX], w_qkv[:, DIM:2 * DIM], xw[:, 0:ROWPIX],
                                     start=True, stop=True).then_inc(s_qk, 1)

                def front_v(g):
                    done(t, s_xw, g)
                    before(t, s_vev, g)
                    for w in range(WIN):
                        base, slot = window(w)
                        mm = nc.tensor.matmul(psum[base:base + 64, 2, slot * DIM:(slot + 1) * DIM],
                                              xw[:, w * TOK:w * TOK + 64],
                                              w_qkv[:, 2 * DIM:3 * DIM], start=True, stop=True)
                    mm.then_inc(s_v, 1)

                def scores(g):
                    done(t, s_qkev, g)
                    before(t, s_sub, g)
                    for w in range(WIN):
                        for h in range(HEADS):
                            r = slice(HEAD_DIM * h, HEAD_DIM * (h + 1))
                            p0, col = 64 * (w % 2), (w // 2) * TOK
                            mm = nc.tensor.matmul(psum[p0:p0 + 64, 3 + h, col:col + TOK],
                                                  qT[r, w * TOK:w * TOK + 64], kT[r, w * TOK:(w + 1) * TOK],
                                                  start=True, stop=True)
                    mm.then_inc(s_score, 1)

                def first(g):
                    before(t, s_trev, g)
                    front_qk(g)
                    front_v(g)
                    scores(g)
                    front_qk(g + 1)
                    front_v(g + 1)

                def step(g, side, row, ahead):
                    if ahead:
                        scores(g + 1)
                    done(t, s_att, g)
                    for n in range(HEADS * PAIRS // 2):
                        mm = nc.tensor.transpose(psum[:, n // 4, n % 4 * 128:(n % 4 + 1) * 128],
                                                 sm[:, side, 2 * n:2 * n + 2, :].rearrange("p t m -> p (t m)"),
                                                 ident[:, :])
                    mm.then_inc(s_tr, 1)
                    if row is not None:
                        front_v(g + 2)
                    done(t, s_trev, g)
                    done(t, s_vev, g)
                    before(t, s_prev, g)
                    t.sem_inc(s_gate, 1)
                    for w in range(WIN):
                        for h in range(HEADS):
                            base, slot = window(w)
                            at = (2 * h) * 128 + slot * 64
                            mm = nc.tensor.matmul(psum[HEAD_DIM * h:HEAD_DIM * (h + 1), 6 + base // 64,
                                                       slot * TOK:(slot + 1) * TOK],
                                                  v_tok[base:base + TOK, side, slot, HEAD_DIM * h:HEAD_DIM * (h + 1)],
                                                  attT[base:base + TOK, at:at + TOK], start=True, stop=True)
                    mm.then_inc(s_o, 1)
                    if row is not None:
                        front_qk(g + 2)
                    done(t, s_oev, g)
                    nc.tensor.matmul(psum[0:DIM, 7, 0:ROWPIX], w_o[:, :], oT[:, :],
                                     start=True, stop=True).then_inc(s_pr, 1)

                def body(i, b, par):
                    before(t, s_prev, b * WIN)
                    gn_tensor(t, b)
                    row_loop(nc.tensor, b, first, step)

                image_loop(nc.tensor, body)

            @block.vector
            def _(v):
                nc.vector.memset(qT[:, ROWPIX:], 0.0)
                nc.vector.memset(sm[:, :, :, :], 0.0)
                nc.vector.memset(xw[:, ROWPIX:], 0.0).then_inc(s_pad, 1)
                nc.vector.memset(eps[:, :], LN_EPS)
                v.wait_ge(s_w, n_w)
                nc.vector.tensor_reduce(d_sum[:, :], d_skip[:, :, :], AX.X, ALU.add).then_inc(s_const, 1)
                v.wait_ge(s_const, 2)
                nc.vector.tensor_scalar(a_neg[:, :, :], a_neg[:, :, :], -1.0, None, ALU.mult).then_inc(s_const, 1)

                def values(g, side):
                    done(v, s_v, g)
                    before(v, s_o, g)
                    nc.vector.tensor_copy(v_tok[:, side, :, :].rearrange("p w c -> p (w c)"),
                                          psum[:, 2, 0:4 * DIM]).then_inc(s_vev, 1)

                def softmax(g, side):
                    p = smt[side]
                    done(v, s_score, g)
                    before(v, s_tr, g)
                    for h in range(HEADS):
                        st = nc.vector.scalar_tensor_tensor(
                            sm[:, side, h * PAIRS:(h + 1) * PAIRS, 0:TOK],
                            psum[:, 3 + h, 0:PAIRS * TOK].rearrange("p (w m) -> p w m", m=TOK), SCALE,
                            pos_bias[:, h:h + 1, :].to_broadcast([128, PAIRS, TOK]), ALU.mult, ALU.add)
                    st.then_inc(s_ss, 1)
                    v.wait_ge(s_ss, g * 4 + 1)
                    nc.vector.tensor_reduce(mx[:, :], p, AX.X, ALU.max).then_inc(s_ss, 1)
                    v.wait_ge(s_ss, g * 4 + 2)
                    nc.vector.tensor_tensor(p, p, mx[:, :].unsqueeze(2).to_broadcast([128, HEADS * PAIRS, TOK]),
                                            ALU.subtract).then_inc(s_sub, 1)
                    done(v, s_exp, g)
                    nc.vector.tensor_reduce(mx[:, :], p, AX.X, ALU.add).then_inc(s_ss, 1)
                    v.wait_ge(s_ss, g * 4 + 3)
                    nc.vector.reciprocal(rs[:, :], mx[:, :]).then_inc(s_ss, 1)
                    v.wait_ge(s_ss, g * 4 + 4)
                    nc.vector.tensor_tensor(p, p, rs[:, :].unsqueeze(2).to_broadcast([128, HEADS * PAIRS, TOK]),
                                            ALU.mult).then_inc(s_att, 1)

                def first(g):
                    values(g, 0)
                    softmax(g, 0)
                    values(g + 1, 1)

                def step(g, side, row, ahead):
                    if ahead:
                        softmax(g + 1, 1 - side)
                    if row is not None:
                        values(g + 2, side)

                def body(i, b, par):
                    def ready():
                        v.wait_ge(s_load[par], i * 16 + 16)
                        before(v, s_xw, b * WIN)
                    gn_vector(v, b, par, ready)
                    row_loop(nc.vector, b, first, step)

                image_loop(nc.vector, body)

            @block.gpsimd
            def _(p):
                def body(i, b, par):
                    with nc.gpsimd.Fori(0, WIN) as hh:
                        g = b * WIN + hh
                        done(p, s_prev, g)
                        r = rows(par, hh, "rows")
                        nc.gpsimd.tensor_tensor(r, r, proj[:, :].rearrange("p (i w) -> p i w", w=SIDE),
                                                ALU.add).then_inc(s_res, 1)

                image_loop(nc.gpsimd, body)

        with ExitStack() as pb:
            def sbb(name, shape, dtype=F32):
                return pb.enter_context(nc.sbuf_tensor(name, shape, dtype))

            def semb(name):
                return pb.enter_context(nc.semaphore(name))

            conv_diag = sbb("conv_diag", [DIM, 9, DIM])
            u = sbb("u", [DIM, HALVES, PIX])
            y = sbb("y", [DIM, HALVES, PIX])
            h = sbb("h", [128, TILES, CH])
            idle = h[0:DIM, :, :].rearrange("p t c -> p (t c)")
            xx = idle[:, 0:HALVES * PADDED * PADDED].rearrange("p (f r w) -> p f r w", f=HALVES, r=PADDED)
            gate = idle[:, 0:HALVES * PIX].rearrange("p (f c) -> p f c", f=HALVES)
            xn = idle[:, 16 * CH:16 * CH + PIX]
            decay = sbb("decay", [128, 6, CH])
            dbu = sbb("dbu", [128, 3, CH])
            hc = sbb("hc", [128, HCS, CH])
            bc = sbb("bc", [128, 2, 8, CH])
            delta = sbb("delta", [DIM, HALVES, 2, CH], F32R)
            du = sbb("du", [DIM, HALVES, 2, CH], F32R)
            xd = sbb("xd", [XD_ROWS, CH])
            xd2 = sbb("xd2", [XD_ROWS, 2, CH], F32R)
            zc = sbb("zc", [DIM, CH])
            ze = sbb("ze", [DIM, CH])
            zl = sbb("zl", [DIM, CH])
            rep_stage = bc[0:DIM, 0, 0, 0:3 * 128]
            bc_stage = bc[0:XD_ROWS, 0, 1:5, :].rearrange("p j c -> p (j c)")[:, 0:8 * 128]
            rstd = bc[0:DIM, 0, 0:CHUNKS, :]
            halves_sum = [hc[0:DIM, 4, :], hc[0:DIM, 5, :]]
            squares = [dbu[0:DIM, 0:2, :], hc[0:DIM, 0:2, :]]

            def rep_delta(g):
                return psum[:, g % 2, 0:CH]

            def rep_du(g):
                return psum[:, 2 + g % 2, 0:CH]

            Y_BANK = [4, 6]
            BC_BANK, P_BANK = 5, 7
            LAG = 7

            s_diag = semb("s_diag")
            s_xn = semb("s_xn")
            s_zero = semb("s_zero")
            s_xx = semb("s_xx")
            s_xxev = semb("s_xxev")
            s_cv = semb("s_cv")
            s_cvd = semb("s_cvd")
            s_cvp = semb("s_cvp")
            s_u = semb("s_u")
            s_us = semb("s_us")
            s_y0 = semb("s_y0")
            s_zz = semb("s_zz")
            s_zev = semb("s_zev")
            s_ys = semb("s_ys")
            s_mean = semb("s_mean")
            s_yc = semb("s_yc")
            s_sq = semb("s_sq")
            s_sqs = semb("s_sqs")
            s_var = semb("s_var")
            s_vs = semb("s_vs")
            s_lv = semb("s_lv")
            s_rr = semb("s_rr")
            s_nrm = semb("s_nrm")
            s_aff = semb("s_aff")
            s_g = semb("s_g")
            s_op = semb("s_op")
            s_fin = semb("s_fin")
            s_rd = semb("s_rd")
            s_ru = semb("s_ru")
            s_da = semb("s_da")
            s_b = semb("s_b")
            s_h = semb("s_h")
            s_hc = semb("s_hc")
            s_sum = semb("s_sum")
            s_yev = semb("s_yev")
            s_pm = semb("s_pm")
            s_pf = semb("s_pf")
            s_bm = semb("s_bm")
            s_bf = semb("s_bf")
            s_xh = semb("s_xh")
            s_dh = semb("s_dh")
            s_dl = semb("s_dl")
            s_uh = semb("s_uh")
            s_ul = semb("s_ul")
            s_stage = semb("s_stage")
            s_sel = semb("s_sel")
            s_zc = semb("s_zc")
            s_ze = semb("s_ze")
            s_zl = semb("s_zl")
            s_du = semb("s_du")
            starts = [(s_xxev, 2), (s_u, 2), (s_zev, 1), (s_mean, 2), (s_yc, 2), (s_var, 2), (s_vs, 2), (s_fin, 2),
                      (s_da, 8), (s_b, 8), (s_h, 6), (s_hc, TILES), (s_sum, HCS), (s_yev, 2), (s_pf, 1), (s_bf, 1),
                      (s_dl, 1), (s_ul, 1)]

            block = pb.enter_context(nc.Block())

            def conv_out(t, c, n):
                return flat(t[:, c * CH:(c + n) * CH])

            def conv_in(f, c, n, tap):
                dr, dc = divmod(tap, 3)
                return xx[:, f, c * LINES + dr:(c + n) * LINES + dr, dc:dc + SIDE]

            TENSOR_CONV = 5
            VECTOR_CONV = [(1, 0, 4), (1, 4, 3), (0, TENSOR_CONV, 1)]
            VECTOR_STEPS = 9 * len(VECTOR_CONV)
            POOL_STEPS = 17

            def chunk_of(t, k, c):
                pos = c if k < 2 else CHUNKS - 1 - c
                if k % 2 == 0:
                    return t[:, bass.ds(pos * CH, CH)].rearrange("p (l s) -> p l s", s=SIDE)
                return t.rearrange("p (h w) -> p w h", w=SIDE)[:, bass.ds(pos * LINES, LINES), :]

            def flat(t):
                return t.rearrange("p (l s) -> p l s", s=SIDE)

            def directed(t, k):
                return t if k < 2 else t[:, ::-1]

            def chunk_loop(eng, b, chunk):
                for k in range(DIRS):
                    base = b * (DIRS * CHUNKS) + k * CHUNKS
                    parity = k * CHUNKS % 2

                    def one(c, back, ahead):
                        chunk(k, c, base + c, (parity + back) % 2, (k, c - 1) if back else before_first,
                              (k, c + 1) if ahead else after_last)

                    before_first = (k - 1, CHUNKS - 1) if k else None
                    after_last = (k + 1, 0) if k + 1 < DIRS else None
                    one(0, 0, True)
                    with eng.Fori(0, (CHUNKS - 3) // 2) as j:
                        one(j * 2 + 1, 1, True)
                        one(j * 2 + 2, 2, True)
                    one(CHUNKS - 2, CHUNKS - 2, True)
                    one(CHUNKS - 1, CHUNKS - 1, False)

            def post_loop(*stages):
                for step in range(CHUNKS + max(behind for behind, _ in stages)):
                    for behind, do in stages:
                        if 0 <= step - behind < CHUNKS:
                            do(step - behind)

            @block.sync
            def _(sp):
                for sem_, n in starts:
                    sp.sem_inc(sem_, n)
                for stage, name in ((rep_stage, "rep_sel"), (bc_stage, "bc_sel")):
                    sp.dma_start(stage, a[name].rearrange("p j m -> p (j m)")).then_inc(s_stage, 16)
                half = images // 2

                def load(par, b, n):
                    sp.wait_ge(s_stored[par], (half + n) * 16)
                    sp.dma_start(image[:, par * PIX:(par + 1) * PIX], a["x1"][b]).then_inc(s_load[par], 16)

                def store(b, par):
                    sp.wait_ge(s_fin, (b + 1) * CHUNKS + 2)
                    sp.dma_start(a["out"][b], img(par)).then_inc(s_stored[par], 16)

                for par in range(2):
                    load(par, par, 0)
                if images > 2:
                    with nc.sync.Fori(0, half - 1) as i:
                        for par in range(2):
                            store(i * 2 + par, par)
                            load(par, i * 2 + 2 + par, i + 1)
                for par in range(2):
                    store(images - 2 + par, par)
                for par in range(2):
                    sp.wait_ge(s_stored[par], 2 * half * 16)

            @block.tensor
            def _(t):
                t.wait_ge(s_sel, 2)
                t.wait_ge(s_diag, 1)

                def project(k, c, P):
                    t.wait_ge(s_pf, P * 3 + 1)
                    for f in range(HALVES):
                        mm = nc.tensor.matmul(flat(psum[0:XD_ROWS, P_BANK, 0:CH]), xproj[:, k, f, :],
                                              chunk_of(u[:, f, :], k, c), start=(f == 0), stop=(f == 1))
                    mm.then_inc(s_pm, 1)

                def project_dt(k, P, f):
                    t.wait_ge(s_pf, P * 3 + f + 2)
                    nc.tensor.matmul(psum[0:DIM, P_BANK, 0:CH], dt_w[:, k, f * DIM:(f + 1) * DIM], xd[:, :],
                                     start=True, stop=True).then_inc(s_pm, 1)

                def spread(P, n):
                    t.wait_ge(s_bf, P * SPREADS + n + 1)
                    t.wait_ge(s_pf, P * 3 + 2)
                    for part in range(2):
                        mm = nc.tensor.matmul(psum[:, BC_BANK, 0:CH], bc_sel[:, SPREAD[n][0], :], xd2[:, part, :],
                                              start=(part == 0), stop=(part == 1))
                    mm.then_inc(s_bm, 1)

                def replicate_delta(P, g):
                    f, quadrant = g // 3, g % 3
                    t.wait_ge(s_dl, P * HALVES + f + 2)
                    t.wait_ge(s_da, P * TILES + g * QUADS + 4)
                    for part in range(2):
                        mm = nc.tensor.matmul(rep_delta(g), rep_sel[:, quadrant, :], delta[:, f, part, :],
                                              start=(part == 0), stop=(part == 1))
                    mm.then_inc(s_rd, 1)

                def replicate_du(P, g):
                    f, quadrant = g // 3, g % 3
                    t.wait_ge(s_ul, P * HALVES + f + 2)
                    t.wait_ge(s_b, P * TILES + g * QUADS + 4)
                    for part in range(2):
                        mm = nc.tensor.matmul(rep_du(g), rep_sel[:, quadrant, :], du[:, f, part, :],
                                              start=(part == 0), stop=(part == 1))
                    mm.then_inc(s_ru, 1)

                def tile_sum(G, q):
                    place = q % (TILES // 2)
                    if place == 0:
                        t.wait_ge(s_yev, G * HALVES + q // (TILES // 2) + 1)
                    t.wait_ge(s_hc, G * TILES + q + 1 + TILES)
                    nc.tensor.matmul(psum[0:DIM, Y_BANK[q // (TILES // 2)], 0:CH], sum_sel[:, place // QUADS, :], hc[:, q % HCS, :],
                                     start=(place == 0), stop=(place == TILES // 2 - 1)).then_inc(s_sum, 1)

                def chunk(k, c, G, par, prev, nxt):
                    for q in range(TILES):
                        if q % QUADS == 3:
                            if q + QUADS < TILES:
                                replicate_du(G, q // QUADS + 1)
                            elif nxt:
                                replicate_du(G + 1, 0)
                        if q % QUADS == 1:
                            if q + QUADS < TILES:
                                replicate_delta(G, q // QUADS + 1)
                            elif nxt:
                                replicate_delta(G + 1, 0)
                        if q >= LAG:
                            tile_sum(G, q - LAG)
                        elif prev:
                            tile_sum(G - 1, q - LAG + TILES)
                        if not nxt:
                            continue
                        if q == PROJ_SLOT:
                            project(*nxt, G + 1)
                        for f in range(HALVES):
                            if q == DT_SLOT[f]:
                                project_dt(nxt[0], G + 1, f)
                        for n in range(SPREADS):
                            if q == SPREAD[n][1]:
                                spread(G + 1, n)
                    if not nxt:
                        for q in range(TILES - LAG, TILES):
                            tile_sum(G, q)

                def body(i, b, par):
                    t.wait_ge(s_pf, b * (DIRS * CHUNKS * 3) + 1)
                    gn_tensor(t, b + images)
                    for n in range(2 * CHUNKS):
                        f, c = 1 - n // CHUNKS, n % CHUNKS
                        if f:
                            t.wait_ge(s_xn, b * 14 + c + 1)
                        t.wait_ge(s_xxev, b * 14 + n + 1)
                        nc.tensor.matmul(psum[0:DIM, n % 2, 0:CH], w_in[:, f * DIM:(f + 1) * DIM],
                                         xn[:, c * CH:(c + 1) * CH], start=True, stop=True).then_inc(s_xx, 1)
                    t.wait_ge(s_xxev, b * 14 + 14 + 2)
                    P = b * (DIRS * CHUNKS)
                    for c in range(TENSOR_CONV):
                        t.wait_ge(s_u, b * TENSOR_CONV + c + 1)
                        for tap in range(9):
                            mm = nc.tensor.matmul(flat(psum[0:DIM, 2 + c % 2, 0:CH]), conv_diag[:, tap, :],
                                                  conv_in(0, c, 1, tap), start=(tap == 0), stop=(tap == 8))
                        mm.then_inc(s_cv, 1)
                        if c == TENSOR_CONV - 2:
                            t.wait_ge(s_us, b * 4 + 1)
                            project(0, 0, P)
                    t.wait_ge(s_u, b * TENSOR_CONV + TENSOR_CONV + 2)
                    t.wait_ge(s_us, b * 4 + 4)
                    for f in range(HALVES):
                        project_dt(0, P, f)
                        for n in range(f * SPREADS // 2, (f + 1) * SPREADS // 2):
                            spread(P, n)
                    replicate_delta(P, 0)
                    replicate_du(P, 0)
                    chunk_loop(nc.tensor, b, chunk)
                    def gates(c):
                        t.wait_ge(s_xn, b * 14 + 7 + c + 1)
                        t.wait_ge(s_zev, b * CHUNKS + c + 1)
                        for f in range(HALVES):
                            mm = nc.tensor.matmul(psum[0:DIM, f, 0:CH],
                                                  w_in[:, INNER + f * DIM:INNER + (f + 1) * DIM],
                                                  xn[:, c * CH:(c + 1) * CH], start=True, stop=True)
                        mm.then_inc(s_zz, 1)

                    def mean(c):
                        t.wait_ge(s_ys, b * CHUNKS + c + 1)
                        t.wait_ge(s_yc, b * CHUNKS + c + 1)
                        nc.tensor.matmul(psum[0:DIM, 4 + 2 * (c % 2), 0:CH], inner_avg[:, :], halves_sum[c % 2],
                                         start=True, stop=True).then_inc(s_mean, 1)

                    def variance(c):
                        t.wait_ge(s_sqs, b * CHUNKS + c + 1)
                        t.wait_ge(s_vs, b * CHUNKS + c + 1)
                        nc.tensor.matmul(psum[0:DIM, 5 + 2 * (c % 2), 0:CH], inner_avg[:, :], squares[c % 2][:, 0, :],
                                         start=True, stop=True).then_inc(s_var, 1)

                    def project_out(c):
                        t.wait_ge(s_g, b * CHUNKS + c + 1)
                        t.wait_ge(s_fin, b * CHUNKS + c + 1)
                        for f in range(HALVES):
                            mm = nc.tensor.matmul(psum[0:DIM, 2 + c % 2, 0:CH], w_out2[:, f, :],
                                                  y[:, f, c * CH:(c + 1) * CH], start=(f == 0), stop=(f == 1))
                        mm.then_inc(s_op, 1)

                    post_loop((0, gates), (0, mean), (1, variance))
                    post_loop((0, project_out))

                image_loop(nc.tensor, body)

            @block.scalar
            def _(s):
                s.wait_ge(s_const, 3)
                s.wait_ge(s_stage, 32)
                nc.scalar.activation(rep_sel[:, :, :].rearrange("p j m -> p (j m)"), rep_stage, ACT.Copy).then_inc(s_sel, 1)
                nc.scalar.activation(bc_sel[:, :, :].rearrange("p j m -> p (j m)"), bc_stage, ACT.Copy).then_inc(s_sel, 1)

                def take_projected(P):
                    s.wait_ge(s_pm, P * 3 + 1)
                    src = psum[0:XD_ROWS, P_BANK, 0:CH]
                    nc.scalar.activation(xd[:, :], src, ACT.Identity, bias=one_row[:, :])
                    nc.scalar.activation(xd2[:, 0, :], src, ACT.Copy).then_inc(s_xh, 1)

                def take_spread(P, par, n):
                    s.wait_ge(s_bm, P * SPREADS + n + 1)
                    nc.scalar.activation(bc[:, par, SPREAD[n][0], :], psum[:, BC_BANK, 0:CH],
                                         ACT.Copy).then_inc(s_bf, 1)

                def softplus(P, f):
                    s.wait_ge(s_pm, P * 3 + f + 2)
                    s.wait_ge(s_ul, P * HALVES + f + 1)
                    nc.scalar.activation(zc[:, :], psum[0:DIM, P_BANK, 0:CH], ACT.Abs).then_inc(s_zc, 1)
                    s.wait_ge(s_zc, P * HALVES + f + 1)
                    nc.scalar.activation(ze[:, :], zc[:, :], ACT.Exp, scale=-1.0).then_inc(s_ze, 1)
                    s.wait_ge(s_ze, P * HALVES + f + 1)
                    nc.scalar.activation(zl[:, :], ze[:, :], ACT.Ln, bias=1.0).then_inc(s_zl, 1)

                def delta_high(P, f):
                    s.wait_ge(s_pf, P * 3 + f + 3)
                    nc.scalar.activation(delta[:, f, 0, :], zc[:, :], ACT.Copy).then_inc(s_dh, 1)

                def du_high(P, f):
                    s.wait_ge(s_du, P * HALVES + f + 1)
                    nc.scalar.activation(du[:, f, 0, :], ze[:, :], ACT.Copy).then_inc(s_uh, 1)

                def chunk(k, c, G, par, prev, nxt):
                    for q in range(TILES):
                        g = q // QUADS
                        s.wait_ge(s_rd, G * DGROUPS + g + 1)
                        s.wait_ge(s_h, G * TILES + q + 1)
                        nc.scalar.activation(decay[:, q % 6, :], rep_delta(g), ACT.Exp,
                                             scale=a_neg[:, k, q:q + 1]).then_inc(s_da, 1)
                        if not nxt:
                            continue
                        for f in range(HALVES):
                            if q - SOFTPLUS == DT_SLOT[f]:
                                softplus(G + 1, f)
                            if q - HIGH == DT_SLOT[f]:
                                s.wait_ge(s_ru, G * DGROUPS + 3 * f + 3)
                                delta_high(G + 1, f)
                            if q - HIGH - 1 == DT_SLOT[f]:
                                du_high(G + 1, f)
                        if q == PROJ_TAKE:
                            take_projected(G + 1)
                        for n in range(SPREADS):
                            if q - SPREAD_TAKE == SPREAD[n][1]:
                                if n == 0:
                                    s.wait_ge(s_hc, (G + 1) * TILES)
                                take_spread(G + 1, 1 - par, n)

                def normalise(par):
                    for c in range(CHUNKS):
                        nc.scalar.activation(xn[:, c * CH:(c + 1) * CH], img(par)[:, c * CH:(c + 1) * CH], ACT.Identity,
                                             bias=gm[:, 3:4], scale=gm[:, 2:3]).then_inc(s_xn, 1)

                def body(i, b, par):
                    gn_scalar(s, b + images)
                    normalise(par)
                    s.wait_ge(s_zero, b + 1)
                    for n in range(2 * CHUNKS):
                        f, c = 1 - n // CHUNKS, n % CHUNKS
                        s.wait_ge(s_xx, b * 14 + n + 1)
                        nc.scalar.activation(xx[:, f, 1 + c * LINES:1 + (c + 1) * LINES, 1:1 + SIDE],
                                             flat(psum[0:DIM, n % 2, 0:CH]), ACT.Copy).then_inc(s_xxev, 1)

                    def from_tensor(c):
                        s.wait_ge(s_cv, b * TENSOR_CONV + c + 1)
                        nc.scalar.activation(u[:, 0, c * CH:(c + 1) * CH], psum[0:DIM, 2 + c % 2, 0:CH],
                                             ACT.Silu, bias=conv_b[:, 0:1]).then_inc(s_u, 1)

                    def from_others(f, c, n):
                        part = u[:, f, c * CH:(c + n) * CH]
                        nc.scalar.activation(part, part, ACT.Silu, bias=conv_b[:, f:f + 1]).then_inc(s_us, 1)

                    def from_vector(n):
                        s.wait_ge(s_cvd, b * VECTOR_STEPS + 9 * n + 9)
                        from_others(*VECTOR_CONV[n])

                    P = b * (DIRS * CHUNKS)
                    from_tensor(0)
                    from_tensor(1)
                    from_vector(0)
                    from_tensor(2)
                    s.wait_ge(s_cvp, (b + 1) * POOL_STEPS)
                    from_others(0, CHUNKS - 1, 1)
                    take_projected(P)
                    from_tensor(3)
                    from_vector(1)
                    from_tensor(4)
                    from_vector(2)
                    nc.scalar.preload_act_table_set(LN_EXP)
                    for f in range(HALVES):
                        n = f * SPREADS // 2
                        softplus(P, f)
                        take_spread(P, 0, n)
                        delta_high(P, f)
                        take_spread(P, 0, n + 1)
                        du_high(P, f)
                        take_spread(P, 0, n + 2)
                        take_spread(P, 0, n + 3)
                    chunk_loop(nc.scalar, b, chunk)
                    s.wait_ge(s_hc, (b + 1) * (DIRS * CHUNKS * TILES) + TILES)
                    normalise(par)

                    def gates(c):
                        s.wait_ge(s_zz, b * CHUNKS + c + 1)
                        nc.scalar.activation(gate[:, :, c * CH:(c + 1) * CH], psum[0:DIM, 0:2, 0:CH],
                                             ACT.Silu).then_inc(s_zev, 1)

                    def square(c):
                        s.wait_ge(s_yc, b * CHUNKS + c + 3)
                        s.wait_ge(s_var, b * CHUNKS + c + 1)
                        nc.scalar.activation(squares[c % 2], y[:, :, c * CH:(c + 1) * CH], ACT.Square).then_inc(s_sq, 1)

                    def affine(c):
                        s.wait_ge(s_nrm, b * CHUNKS + c + 1)
                        for f in range(HALVES):
                            yf = y[:, f, c * CH:(c + 1) * CH]
                            ins = nc.scalar.activation(yf, yf, ACT.Identity, bias=ln_b[:, f:f + 1],
                                                       scale=ln_w[:, f:f + 1])
                        ins.then_inc(s_aff, 1)

                    def log_variance(c):
                        s.wait_ge(s_vs, b * CHUNKS + c + 3)
                        nc.scalar.activation(rstd[:, c, :], rstd[:, c, :], ACT.Ln, bias=eps[0:DIM, :]).then_inc(s_lv, 1)

                    def one_over_std(c):
                        s.wait_ge(s_lv, b * CHUNKS + c + 1)
                        nc.scalar.activation(rstd[:, c, :], rstd[:, c, :], ACT.Exp, scale=-0.5).then_inc(s_rr, 1)

                    post_loop((0, gates), (0, square))
                    nc.scalar.preload_act_table_set(LN_EXP)
                    post_loop((0, log_variance), (1, one_over_std), (4, affine))

                image_loop(nc.scalar, body)

            @block.vector
            def _(v):
                for tap in range(9):
                    ins = nc.vector.tensor_scalar(conv_diag[:, tap, :], ident[0:DIM, 0:DIM], conv_w[:, 0, tap:tap + 1],
                                                  None, ALU.mult)
                ins.then_inc(s_diag, 1)
                v.wait_ge(s_const, 3)

                def xd_low(P):
                    v.wait_ge(s_xh, P + 1)
                    nc.vector.tensor_tensor(xd2[:, 1, :], psum[0:XD_ROWS, P_BANK, 0:CH],
                                            xd2[:, 0, :].bitcast(F32), ALU.subtract).then_inc(s_pf, 1)

                def make_delta(P, f):
                    v.wait_ge(s_zl, P * HALVES + f + 1)
                    nc.vector.scalar_tensor_tensor(zc[:, :], psum[0:DIM, P_BANK, 0:CH], 0.0, zl[:, :],
                                                   ALU.max, ALU.add).then_inc(s_pf, 1)

                def make_du(k, c, P, f):
                    v.wait_ge(s_pf, P * 3 + f + 3)
                    nc.vector.tensor_tensor(flat(ze[:, :]), flat(zc[:, :]), chunk_of(u[:, f, :], k, c),
                                            ALU.mult).then_inc(s_du, 1)

                def times_b(G, par, q):
                    g, j = divmod(q, QUADS)
                    if q == 0:
                        v.wait_ge(s_bf, (G + 1) * SPREADS + 1)
                    v.wait_ge(s_ru, G * DGROUPS + g + 1)
                    v.wait_ge(s_h, G * TILES + q + 4)
                    nc.vector.tensor_tensor(dbu[:, q % 3, :], rep_du(g), bc[:, par, j, :], ALU.mult).then_inc(s_b, 1)

                def add_half(k, c, G, f):
                    yk = chunk_of(y[:, f, :], k, c)
                    v.wait_ge(s_sum, G * TILES + (f + 1) * TILES // 2 + HCS)
                    v.sem_inc(s_gate, 1)
                    nc.vector.tensor_tensor(yk, flat(psum[0:DIM, Y_BANK[f], 0:CH]), yk, ALU.add).then_inc(s_yev, 1)

                def chunk(k, c, G, par, prev, nxt):
                    edge = CH - 1 if k < 2 else 0
                    for q in range(TILES):
                        if q + 1 < TILES:
                            times_b(G, par, q + 1)
                        elif nxt:
                            times_b(G + 1, 1 - par, 0)
                        v.wait_ge(s_da, G * TILES + q + 1 + 8)
                        v.wait_ge(s_b, G * TILES + q + 1 + 8)
                        v.wait_ge(s_hc, G * TILES + q + 1)
                        nc.vector.tensor_tensor_scan(directed(h[:, q, :], k), directed(decay[:, q % 6, :], k),
                                                     directed(dbu[:, q % 3, :], k),
                                                     0.0 if isinstance(c, int) and c == 0 else h[:, q, edge:edge + 1],
                                                     ALU.mult, ALU.add).then_inc(s_h, 1)
                        if nxt:
                            for f in range(HALVES):
                                if q - DELTA == DT_SLOT[f]:
                                    make_delta(G + 1, f)
                                if q - DU == DT_SLOT[f]:
                                    make_du(*nxt, G + 1, f)
                            if q == PROJ_LOW:
                                xd_low(G + 1)
                        if q == TILES // 2 + 6:
                            add_half(k, c, G, 0)
                        if q == 6 and prev:
                            add_half(*prev, G - 1, 1)
                    if not nxt:
                        add_half(k, c, G, 1)

                def body(i, b, par):
                    half = images // 2

                    def ready():
                        v.wait_ge(s_load[par], (half + 1 + i) * 16)
                    gn_vector(v, b + images, par, ready)
                    v.wait_ge(s_zero, b + 1)
                    v.wait_ge(s_xxev, b * 14 + 7 + 2)
                    for n in range(VECTOR_STEPS):
                        tap, (f, c, length) = n % 9, VECTOR_CONV[n // 9]
                        out, src, w = conv_out(u[:, f, :], c, length), conv_in(f, c, length, tap), conv_w[:, f, tap:tap + 1]
                        if n == 18:
                            v.wait_ge(s_xxev, b * 14 + 14 + 2)
                        if tap:
                            v.wait_ge(s_cvd, b * VECTOR_STEPS + n)
                            nc.vector.scalar_tensor_tensor(out, src, w, out, ALU.mult, ALU.add).then_inc(s_cvd, 1)
                        else:
                            nc.vector.tensor_scalar(out, src, w, None, ALU.mult).then_inc(s_cvd, 1)
                    P = b * (DIRS * CHUNKS)
                    xd_low(P)
                    v.wait_ge(s_us, b * 4 + 4)
                    v.wait_ge(s_u, b * TENSOR_CONV + TENSOR_CONV + 2)
                    for f in range(HALVES):
                        nc.vector.tensor_scalar(y[:, f, :], u[:, f, :], d_sum[:, f:f + 1], None, ALU.mult).then_inc(s_y0, 1)
                        make_delta(P, f)
                        make_du(0, 0, P, f)
                    v.wait_ge(s_y0, b * 2 + 2)
                    times_b(P, 0, 0)
                    chunk_loop(nc.vector, b, chunk)
                    def centre(c):
                        cs = slice(c * CH, (c + 1) * CH)
                        v.wait_ge(s_mean, b * CHUNKS + c + 3)
                        nc.vector.tensor_tensor(
                            y[:, :, cs], y[:, :, cs],
                            psum[0:DIM, 4 + 2 * (c % 2), 0:CH].unsqueeze(1).to_broadcast([DIM, HALVES, CH]),
                            ALU.subtract).then_inc(s_yc, 1)

                    def keep_variance(c):
                        v.wait_ge(s_var, b * CHUNKS + c + 3)
                        nc.vector.tensor_copy(rstd[:, c, :], psum[0:DIM, 5 + 2 * (c % 2), 0:CH]).then_inc(s_vs, 1)

                    def times_gate(c):
                        cs = slice(c * CH, (c + 1) * CH)
                        v.wait_ge(s_aff, b * CHUNKS + c + 1)
                        nc.vector.tensor_tensor(y[:, :, cs], y[:, :, cs], gate[:, :, cs], ALU.mult).then_inc(s_g, 1)

                    def add_squares(c):
                        v.wait_ge(s_sq, b * CHUNKS + c + 1)
                        sq = squares[c % 2]
                        nc.vector.tensor_tensor(sq[:, 0, :], sq[:, 0, :], sq[:, 1, :], ALU.add).then_inc(s_sqs, 1)

                    def residual(c):
                        v.wait_ge(s_op, b * CHUNKS + c + 1)
                        x = img(par)[:, c * CH:(c + 1) * CH]
                        nc.vector.tensor_tensor(x, psum[0:DIM, 2 + c % 2, 0:CH], x, ALU.add).then_inc(s_fin, 1)

                    post_loop((0, centre), (1, keep_variance), (0, add_squares))
                    post_loop((0, times_gate), (2, residual))

                image_loop(nc.vector, body)

            @block.gpsimd
            def _(p):
                def delta_low(P, f):
                    p.wait_ge(s_dh, P * HALVES + f + 1)
                    nc.gpsimd.tensor_tensor(delta[:, f, 1, :], zc[:, :], delta[:, f, 0, :].bitcast(F32),
                                            ALU.subtract).then_inc(s_dl, 1)

                def du_low(P, f):
                    p.wait_ge(s_uh, P * HALVES + f + 1)
                    nc.gpsimd.tensor_tensor(du[:, f, 1, :], ze[:, :], du[:, f, 0, :].bitcast(F32),
                                            ALU.subtract).then_inc(s_ul, 1)

                def chunk(k, c, G, par, prev, nxt):
                    p.wait_ge(s_bf, (G + 1) * SPREADS + 1)
                    for q in range(TILES):
                        p.wait_ge(s_h, G * TILES + q + 1 + 6)
                        p.wait_ge(s_sum, G * TILES + q + 1)
                        nc.gpsimd.tensor_tensor(hc[:, q % HCS, :], h[:, q, :], bc[:, par, 4 + q % QUADS, :],
                                                ALU.mult).then_inc(s_hc, 1)
                        if nxt:
                            for f in range(HALVES):
                                if q - LOW == DT_SLOT[f]:
                                    delta_low(G + 1, f)
                                if q - LOW - 1 == DT_SLOT[f]:
                                    du_low(G + 1, f)

                def body(i, b, par):
                    p.wait_ge(s_fin, b * CHUNKS + 2)
                    p.sem_inc(s_gate, 1)
                    nc.gpsimd.memset(xx[:, :, 0:PADDED:PADDED - 1, :], 0.0)
                    nc.gpsimd.memset(xx[:, :, 1:1 + SIDE, 0:PADDED:PADDED - 1], 0.0).then_inc(s_zero, 1)
                    p.wait_ge(s_xxev, b * 14 + 14 + 2)
                    p.sem_inc(s_gate, 1)
                    out = conv_out(u[:, 0, :], CHUNKS - 1, 1)
                    product = flat(hc[0:DIM, 0, :])
                    for tap in range(9):
                        src = conv_in(0, CHUNKS - 1, 1, tap)
                        if tap > 1:
                            p.wait_ge(s_cvp, b * POOL_STEPS + 2 * tap - 1)
                            p.sem_inc(s_gate, 1)
                        nc.gpsimd.tensor_scalar(product if tap else out, src, conv_w[:, 0, tap:tap + 1], None,
                                                ALU.mult).then_inc(s_cvp, 1)
                        if tap:
                            p.wait_ge(s_cvp, b * POOL_STEPS + 2 * tap)
                            nc.gpsimd.tensor_tensor(out, out, product, ALU.add).then_inc(s_cvp, 1)
                    P = b * (DIRS * CHUNKS)
                    for f in range(HALVES):
                        delta_low(P, f)
                        du_low(P, f)
                    chunk_loop(nc.gpsimd, b, chunk)

                    def add_halves(c):
                        p.wait_ge(s_mean, b * CHUNKS + c + 1)
                        nc.gpsimd.tensor_tensor(halves_sum[c % 2], y[:, 0, c * CH:(c + 1) * CH],
                                                y[:, 1, c * CH:(c + 1) * CH], ALU.add).then_inc(s_ys, 1)

                    def times_std(c):
                        cs = slice(c * CH, (c + 1) * CH)
                        p.wait_ge(s_rr, b * CHUNKS + c + 1)
                        nc.gpsimd.tensor_tensor(y[:, :, cs], y[:, :, cs],
                                                rstd[:, c:c + 1, :].to_broadcast([DIM, HALVES, CH]),
                                                ALU.mult).then_inc(s_nrm, 1)

                    p.wait_ge(s_yev, (b + 1) * 2 * DIRS * CHUNKS + 2)
                    post_loop((0, add_halves))
                    post_loop((0, times_std))

                image_loop(nc.gpsimd, body)


def selectors():
    rep = np.zeros((DIM, 3, 128), np.float32)
    bc = np.zeros((XD_ROWS, 8, 128), np.float32)
    total = np.zeros((128, 3, DIM), np.float32)
    for m in range(128):
        for quadrant in range(3):
            rep[32 * quadrant + m % 32, quadrant, m] = 1
        for j in range(4):
            bc[B_ROW + 4 * j + m // 32, j, m] = 1
            bc[C_ROW + 4 * j + m // 32, 4 + j, m] = 1
        for quadrant in range(3):
            total[m, quadrant, 32 * quadrant + m % 32] = 1
    groups = np.arange(DIM) // GROUP
    return {"rep_sel": rep, "bc_sel": bc, "sum_sel": total, "ident": np.eye(128, dtype=np.float32),
            "group_avg": (groups[:, None] == groups[None, :]).astype(np.float32) / np.float32(GROUP),
            "inner_avg": np.full((DIM, DIM), 1 / INNER, np.float32)}


def position_index():
    i, j = np.divmod(np.arange(TOK), WS)
    return (i[:, None] - i[None, :] + WS - 1) * (2 * WS - 1) + j[:, None] - j[None, :] + WS - 1


def layouts(inputs):
    g = {k: np.asarray(v) for k, v in inputs.items()}
    images = g["x"].shape[0]

    def halves(v):
        return v.reshape(HALVES, DIM).T

    bias = np.zeros((2, 64, HEADS, TOK), np.float32)
    bias[:, :TOK] = g["L0_conv_rel_pos"][:, position_index()].transpose(1, 0, 2)
    xproj = np.zeros((DIM, DIRS, HALVES, XD_ROWS), np.float32)
    w = g["L1_conv_x_proj_weight"].reshape(DIRS, RANK + 2 * STATE, HALVES, DIM).transpose(3, 0, 2, 1)
    xproj[..., 0:RANK] = w[..., 0:RANK]
    xproj[..., B_ROW:B_ROW + STATE] = w[..., RANK:RANK + STATE]
    xproj[..., C_ROW:C_ROW + STATE] = w[..., RANK + STATE:]
    dt_w = np.zeros((XD_ROWS, DIRS, INNER), np.float32)
    dt_w[0:RANK] = g["L1_conv_dt_projs_weight"].transpose(2, 0, 1)
    dt_w[ONE_ROW] = g["L1_conv_dt_projs_bias"]
    one_row = np.zeros((XD_ROWS, 1), np.float32)
    one_row[ONE_ROW] = 1
    a_log = g["L1_conv_A_logs"].reshape(DIRS, DGROUPS, 32, QUADS, 4).transpose(4, 2, 0, 1, 3)
    return selectors() | {
        "x": g["x"].reshape(images, PIX, DIM).transpose(0, 2, 1),
        "w_qkv": g["L0_conv_w_qkv"], "b_qkv": g["L0_conv_b_qkv"].reshape(3, DIM).T,
        "w_o": g["L0_conv_w_out"], "b_o": g["L0_conv_b_out"].reshape(DIM, 1),
        "pos_bias": bias.reshape(128, HEADS, TOK),
        "w_in": g["L1_conv_in_proj_w"].T,
        "conv_w": g["L1_conv_conv_w"].reshape(HALVES, DIM, 9).transpose(1, 0, 2),
        "conv_b": halves(g["L1_conv_conv_b"]),
        "xproj": xproj,
        "dt_w": dt_w,
        "one_row": one_row,
        "a_log": a_log.reshape(128, DIRS, TILES),
        "d_skip": g["L1_conv_Ds"].reshape(DIRS, HALVES, DIM).transpose(2, 1, 0),
        "ln_w": halves(g["L1_conv_ln_w"]), "ln_b": halves(g["L1_conv_ln_b"]),
        "w_out2": g["L1_conv_out_proj_w"].reshape(DIM, HALVES, DIM).transpose(2, 1, 0),
    }


def program(nc, arrays, images):
    a = {n: nc.dram_tensor(f"in_{n}", v.shape, F32, kind="ExternalInput").ap() for n, v in arrays.items()}
    a["x1"] = nc.dram_tensor("x1", (images, DIM, PIX), F32, kind="Internal").ap()
    a["out"] = nc.dram_tensor("out", (images, DIM, PIX), F32, kind="ExternalOutput").ap()
    build(nc, a, images)


def kernel(**inputs):
    from concourse import bacc
    from concourse.bass_utils import run_bass_kernel_spmd

    arrays = {n: np.ascontiguousarray(v) for n, v in layouts(inputs).items()}
    images = arrays["x"].shape[0]
    nc = bacc.Bacc("TRN2", target_bir_lowering=False, num_devices=1, dynamic_dma_scratch_size=1024)
    program(nc, arrays, images)
    r = run_bass_kernel_spmd(nc, [{f"in_{n}": v for n, v in arrays.items()}], core_ids=[0])
    out = r.results[0]["out"]
    return np.ascontiguousarray(out.transpose(0, 2, 1)).reshape(images, SIDE, SIDE, DIM)
```
